# Optimizing a Trainium2 kernel written in Bass

```python
import numpy as np
import jax
import jax.numpy as jnp

def _softmax(x, axis=-1):
    return jax.nn.softmax(x, axis=axis)

def _gelu(x):
    return jax.nn.gelu(x, approximate=True)

def _silu(x):
    return jax.nn.silu(x)

def _sigmoid(x):
    return jax.nn.sigmoid(x)

def _layernorm(x, axis=-1, eps=1e-05):
    m = jnp.mean(x, axis=axis, keepdims=True)
    v = jnp.var(x, axis=axis, keepdims=True)
    return (x - m) / jnp.sqrt(v + eps)

def _scatter_add(tgt, idx, src, axis=0):
    return tgt.at[idx].add(src)

def _segment_sum(src, seg, n):
    return jax.ops.segment_sum(src, seg, n)
kernel_name = 'mk_hybrid_d1_jaxref_r4_2da719'

def setup_inputs(seed: int=0):
    np.random.seed(seed)
    _w = jnp.asarray

    def _L0_attn_a_setup():
        import jax, jax.numpy as jnp
        import numpy as np
        import math
        DIM = 256
        NUM_HEADS = 16
        HEAD_DIM = DIM // NUM_HEADS
        MAX_BIAS = 8.0
        SCALE = HEAD_DIM ** (-0.5)

        def _alibi_slopes(n):

            def pow2(n):
                start = 2.0 ** (-2.0 ** (-(math.log2(n) - 3)))
                return [start * start ** i for i in range(n)]
            if math.log2(n).is_integer():
                return pow2(n)
            c = 2 ** math.floor(math.log2(n))
            return pow2(c) + _alibi_slopes(2 * c)[0::2][:n - c]

        def _rotate_half(t):
            t1, t2 = jnp.split(t, 2, axis=-1)
            return jnp.concatenate([-t2, t1], axis=-1)
        key = jax.random.key(seed)
        k1, k2, k3, k4 = jax.random.split(key, 4)
        B, N, C = (2, 512, DIM)
        x = jax.random.normal(k1, (B, N, C), dtype=jnp.float32)
        qkv_w = jax.random.normal(k2, (3 * C, C), dtype=jnp.float32) * C ** (-0.5)
        proj_w = jax.random.normal(k3, (C, C), dtype=jnp.float32) * C ** (-0.5)
        proj_b = jax.random.normal(k4, (C,), dtype=jnp.float32) * 0.01
        slopes = jnp.asarray(np.array(_alibi_slopes(NUM_HEADS), dtype=np.float32))
        return {'x': x, 'qkv_w': qkv_w, 'proj_w': proj_w, 'proj_b': proj_b, 'slopes': slopes}
    _L0_attn_a_in = _L0_attn_a_setup()

    def _L0_attn_b_setup():
        import jax, jax.numpy as jnp
        import numpy as np
        EMBED_DIM = 256
        NUM_HEADS = 16
        HEAD_DIM = EMBED_DIM // NUM_HEADS
        BATCH, SEQ = (2, 256)
        key = jax.random.key(seed)
        k1, k2, k3, k4, k5 = jax.random.split(key, 5)
        x = jax.random.normal(k1, (BATCH, SEQ, EMBED_DIM), dtype=jnp.float32)
        proj_w = jax.random.normal(k2, (EMBED_DIM, EMBED_DIM), dtype=jnp.float32) / np.sqrt(EMBED_DIM)
        proj_b = jax.random.normal(k3, (EMBED_DIM,), dtype=jnp.float32) * 0.01
        wq = jax.random.normal(k4, (NUM_HEADS, HEAD_DIM, HEAD_DIM), dtype=jnp.float32) / np.sqrt(HEAD_DIM)
        wk = jax.random.normal(k5, (NUM_HEADS, HEAD_DIM, HEAD_DIM), dtype=jnp.float32) / np.sqrt(HEAD_DIM)
        return {'x': x, 'proj_w': proj_w, 'proj_b': proj_b, 'wq': wq, 'wk': wk}
    _L0_attn_b_in = _L0_attn_b_setup()

    def _L0_ffn_setup():
        import jax, jax.numpy as jnp
        import numpy as np
        CAPACITY_FACTOR = 0.5
        key = jax.random.key(seed)
        ks = jax.random.split(key, 5)
        B, S, D, F = (4, 1024, 256, 1024)
        scale_in = 1.0 / np.sqrt(D)
        scale_ff = 1.0 / np.sqrt(F)
        return {'hidden_states': jax.random.normal(ks[0], (B, S, D), dtype=jnp.float32), 'w_router': jax.random.normal(ks[1], (D,), dtype=jnp.float32) * scale_in, 'W1': jax.random.normal(ks[2], (D, F), dtype=jnp.float32) * scale_in, 'b1': jnp.zeros((F,), dtype=jnp.float32), 'W2': jax.random.normal(ks[3], (F, D), dtype=jnp.float32) * scale_ff, 'b2': jnp.zeros((D,), dtype=jnp.float32)}
    _L0_ffn_in = _L0_ffn_setup()
    _d = {'L0_attn_a_x': _L0_attn_a_in['x'], 'L0_attn_a_qkv_w': _L0_attn_a_in['qkv_w'], 'L0_attn_a_proj_w': _L0_attn_a_in['proj_w'], 'L0_attn_a_proj_b': _L0_attn_a_in['proj_b'], 'L0_attn_a_slopes': _L0_attn_a_in['slopes'], 'L0_attn_b_proj_w': _L0_attn_b_in['proj_w'], 'L0_attn_b_proj_b': _L0_attn_b_in['proj_b'], 'L0_attn_b_wq': _L0_attn_b_in['wq'], 'L0_attn_b_wk': _L0_attn_b_in['wk'], 'L0_ffn_w_router': _L0_ffn_in['w_router'], 'L0_ffn_W1': _L0_ffn_in['W1'], 'L0_ffn_b1': _L0_ffn_in['b1'], 'L0_ffn_W2': _L0_ffn_in['W2'], 'L0_ffn_b2': _L0_ffn_in['b2']}
    _x0 = _d['L0_attn_a_x']
    _d['L0_attn_a_x'] = jax.random.normal(jax.random.fold_in(jax.random.key(seed), 1), (2, 2048, 256), dtype=_x0.dtype)
    del _x0
    return _d

def reference(L0_attn_a_x, L0_attn_a_qkv_w, L0_attn_a_proj_w, L0_attn_a_proj_b, L0_attn_a_slopes, L0_attn_b_proj_w, L0_attn_b_proj_b, L0_attn_b_wq, L0_attn_b_wk, L0_ffn_w_router, L0_ffn_W1, L0_ffn_b1, L0_ffn_W2, L0_ffn_b2):

    def _L0_attn_a_ref(x, qkv_w, proj_w, proj_b, slopes):
        import jax, jax.numpy as jnp
        import numpy as np
        import math
        DIM = 256
        NUM_HEADS = 16
        HEAD_DIM = DIM // NUM_HEADS
        MAX_BIAS = 8.0
        SCALE = HEAD_DIM ** (-0.5)

        def _alibi_slopes(n):

            def pow2(n):
                start = 2.0 ** (-2.0 ** (-(math.log2(n) - 3)))
                return [start * start ** i for i in range(n)]
            if math.log2(n).is_integer():
                return pow2(n)
            c = 2 ** math.floor(math.log2(n))
            return pow2(c) + _alibi_slopes(2 * c)[0::2][:n - c]

        def _rotate_half(t):
            t1, t2 = jnp.split(t, 2, axis=-1)
            return jnp.concatenate([-t2, t1], axis=-1)
        B, N, C = x.shape
        H, D = (NUM_HEADS, HEAD_DIM)
        qkv = (x @ qkv_w.T).reshape(B, N, 3, H, D).transpose(2, 0, 3, 1, 4)
        q, k, v = (qkv[0], qkv[1], qkv[2])
        inv_freq = 1.0 / 10000.0 ** (jnp.arange(0, D, 2, dtype=jnp.float32) / D)
        freqs = jnp.arange(N, dtype=jnp.float32)[:, None] * inv_freq[None, :]
        sin = jnp.tile(jnp.sin(freqs), (1, 2))
        cos = jnp.tile(jnp.cos(freqs), (1, 2))
        q = q * cos + _rotate_half(q) * sin
        k = k * cos + _rotate_half(k) * sin
        attn = jnp.einsum('bhqd,bhkd->bhqk', q, k) * SCALE
        pos = jnp.arange(N, dtype=jnp.float32)
        diff = pos[None, :] - pos[:, None]
        diff = jnp.where(diff > 0, 0.0, diff)
        alibi = diff[None, :, :] * slopes[:, None, None] * MAX_BIAS
        attn = attn + alibi[None]
        w = jax.nn.softmax(attn, axis=-1)
        out = jnp.einsum('bhqk,bhkd->bhqd', w, v)
        out = out.transpose(0, 2, 1, 3).reshape(B, N, C)
        return out @ proj_w.T + proj_b

    def _L0_attn_b_ref(x, proj_w, proj_b, wq, wk):
        import jax, jax.numpy as jnp
        import numpy as np
        EMBED_DIM = 256
        NUM_HEADS = 16
        HEAD_DIM = EMBED_DIM // NUM_HEADS
        BATCH, SEQ = (2, 256)
        B, S, D = x.shape
        H, hd = (NUM_HEADS, HEAD_DIM)
        proj = jnp.einsum('bsd,ed->bse', x, proj_w) + proj_b
        flat = jnp.transpose(proj.reshape(B, S, H, hd), (2, 0, 1, 3)).reshape(H, B * S, hd)
        q = jnp.einsum('hnd,hde->hne', flat, wq)
        k = jnp.einsum('hnd,hde->hne', flat, wk)
        logits = jnp.einsum('hne,hme->hnm', q, k) / jnp.sqrt(jnp.asarray(D, x.dtype))
        attn = jax.nn.softmax(logits, axis=-1)
        out = jnp.einsum('hnm,hmd->hnd', attn, flat)
        out = jnp.transpose(out.reshape(H, B, S, hd), (1, 2, 0, 3)).reshape(B, S, D)
        return out

    def _L0_ffn_ref(hidden_states, w_router, W1, b1, W2, b2):
        import jax, jax.numpy as jnp
        import numpy as np
        CAPACITY_FACTOR = 0.5
        'Mixture-of-Depths block: route top-k tokens through an FFN inner block,\n            scatter back with sigmoid router weights; bypassed tokens pass through.'
        B, S, D = hidden_states.shape
        k = int(S * CAPACITY_FACTOR)
        scores = jnp.einsum('bsd,d->bs', hidden_states, w_router)
        top_scores, top_idx = jax.lax.top_k(scores, k)
        weights = jax.nn.sigmoid(top_scores)
        selected = jnp.take_along_axis(hidden_states, top_idx[:, :, None], axis=1)
        h = jax.nn.gelu(jnp.einsum('bkd,df->bkf', selected, W1) + b1)
        processed = jnp.einsum('bkf,fd->bkd', h, W2) + b2
        update = weights[:, :, None] * processed

        def scatter_one(xb, ib, ub):
            return xb.at[ib].add(ub)
        output = jax.vmap(scatter_one)(hidden_states, top_idx, update)
        return output
    x = L0_attn_a_x
    x = x + _L0_attn_a_ref(_layernorm(x, axis=-1), L0_attn_a_qkv_w, L0_attn_a_proj_w, L0_attn_a_proj_b, L0_attn_a_slopes)
    x = x + _L0_ffn_ref(_layernorm(x, axis=-1), L0_ffn_w_router, L0_ffn_W1, L0_ffn_b1, L0_ffn_W2, L0_ffn_b2)
    x = x + _L0_attn_b_ref(_layernorm(x, axis=-1), L0_attn_b_proj_w, L0_attn_b_proj_b, L0_attn_b_wq, L0_attn_b_wk)
    x = x + _L0_ffn_ref(_layernorm(x, axis=-1), L0_ffn_w_router, L0_ffn_W1, L0_ffn_b1, L0_ffn_W2, L0_ffn_b2)
    return x

_drawn_inputs = setup_inputs


def setup_inputs(seed=0):
    import zlib

    import numpy as np

    out = dict(_drawn_inputs(seed))
    spreads = {'L0_ffn_b1': (0.0, 0.298), 'L0_ffn_b2': (0.0, 0.1)}
    factors = {'L0_attn_a_proj_b': 5.675, 'L0_attn_b_proj_b': 8.0}
    for name, (base, spread) in spreads.items():
        noise = np.random.default_rng([zlib.crc32(name.encode()), seed]).standard_normal(out[name].shape)
        drawn = base * np.exp(spread * noise) if base else spread * noise
        out[name] = jnp.asarray(drawn.astype(out[name].dtype))
    for name, factor in factors.items():
        out[name] = (out[name] * factor).astype(out[name].dtype)
    return out
```

```python
import math
from contextlib import ExitStack, contextmanager

import numpy as np

import concourse.bass as bass
from concourse import mybir

F32 = mybir.dt.float32
BF16 = mybir.dt.bfloat16
I32 = mybir.dt.int32
U32 = mybir.dt.uint32
ALU = mybir.AluOpType
ACT = mybir.ActivationFunctionType
AX = mybir.AxisListType

P = 128
BATCH, SEQ, DM = 2, 2048, 256
TOK = BATCH * SEQ
NT = TOK // P
HEADS, HD = 16, 16
DH = DM // P
FF = 1024
KEEP = SEQ // 2
SLOTS = BATCH * KEEP
CHUNK = 512
NCHUNK = TOK // CHUNK
EPS = 1e-5

Q_PARTS = (0, 0, 0, 1, 1, 2)
K_PARTS = (0, 1, 2, 0, 1, 0)
ROWS = HD * len(Q_PARTS)
ROWS_Q = ROWS + 3
STORED = 3 * HD

UNIT_Q = 2048
QC = UNIT_Q // CHUNK
VW = 32
GROUP = 3
P_SLOTS = 4
LEAD = 2


def groups_of(tiles):
    n = -(-tiles // GROUP)
    n += -n % 2
    twos = GROUP * n - tiles
    return [GROUP] * (n - twos) + [GROUP - 1] * twos


def transpose_steps(pe, act, src, dst, ident, psum, tiles, src_ready, copied, done):
    steps = [(quad, half) for quad in range(tiles // 4) for half in range(DH)]

    def on_pe():
        for n, (quad, half) in enumerate(steps):
            if half == 0:
                src_ready(pe, quad)
            if n >= 4:
                pe.wait_ge(copied, n - 3)
            for j in range(4):
                last = pe.matmul(psum[:, n % 4, P * j:P * (j + 1)],
                                 src[:, 4 * quad + j, P * half:P * (half + 1)], ident[:, :],
                                 is_transpose=True, start=True, stop=True)
            last.then_inc(done, 1)

    def on_act():
        for n, (quad, half) in enumerate(steps):
            act.wait_ge(done, n + 1)
            act.activation(dst[:, half, CHUNK * quad:CHUNK * (quad + 1)], psum[:, n % 4, :],
                           ACT.Copy).then_inc(copied, 1)

    return on_pe, on_act, len(steps)


@contextmanager
def semaphores(nc, phase):
    taken = []

    def sem(name):
        taken.append(nc.alloc_semaphore(f"{phase}_{name}"))
        return taken[-1]

    yield sem
    nc.clear_and_free_semaphores(taken)
    nc.all_engine_barrier()


class Shared:
    pass


def layer_norm(nc, sh, name, hs, hT):
    GT = 8
    with ExitStack() as ctx:
        sb = lambda n, s, d: ctx.enter_context(nc.sbuf_tensor(f"{name}_{n}", s, d))
        sem = ctx.enter_context(semaphores(nc, name))
        stats = sb("stats", [P, NT, 6], F32)
        mv = sb("mv", [P, NT, 2], F32)
        var = sb("var", [P, NT], F32)
        std = sb("std", [P, NT], F32)
        rstd = sb("rstd", [P, NT], F32)
        psum = ctx.enter_context(nc.psum_tensor(f"{name}_ps", [P, 4, CHUNK], F32))
        stats_done, mv_done, var_done, std_done = sem("stats"), sem("mv"), sem("var"), sem("std")
        rstd_done, hs_done, copied, transposed = sem("rstd"), sem("hs"), sem("copied"), sem("tr")
        block = ctx.enter_context(nc.Block())

        @block.vector
        def _(dve):
            for g in range(NT // GT):
                span = slice(GT * g, GT * (g + 1))
                for t in range(GT * g, GT * (g + 1)):
                    dve.bn_stats(stats[:, t, :], sh.x[:, t, :]).then_inc(stats_done, 1)
                dve.wait_ge(stats_done, GT * (g + 1))
                for t in range(GT * g, GT * (g + 1)):
                    dve.bn_aggr(mv[:, t, :], stats[:, t, :]).then_inc(mv_done, 1)
                dve.wait_ge(mv_done, GT * (g + 1))
                dve.tensor_scalar(var[:, span], mv[:, span, 1], EPS, None, ALU.add).then_inc(var_done, 1)
            for g in range(NT // GT):
                span = slice(GT * g, GT * (g + 1))
                dve.wait_ge(std_done, g + 1)
                dve.reciprocal(rstd[:, span], std[:, span]).then_inc(rstd_done, 1)
                dve.wait_ge(rstd_done, g + 1)
                for t in range(GT * g, GT * (g + 1)):
                    dve.tensor_scalar(hs[:, t, :], sh.x[:, t, :], mv[:, t, 0:1], rstd[:, t:t + 1],
                                      ALU.subtract, ALU.mult).then_inc(hs_done, 1)

        def hs_ready(pe, quad):
            pe.wait_ge(hs_done, 4 * (quad + 1))

        @block.tensor
        def _(pe):
            on_pe, _, _ = transpose_steps(pe, None, hs, hT, sh.ident, psum, NT, hs_ready, copied, transposed)
            on_pe()

        @block.scalar
        def _(act):
            for g in range(NT // GT):
                span = slice(GT * g, GT * (g + 1))
                act.wait_ge(var_done, g + 1)
                act.activation(std[:, span], var[:, span], ACT.Sqrt).then_inc(std_done, 1)
            _, on_act, _ = transpose_steps(None, act, hs, hT, sh.ident, psum, NT, hs_ready, copied, transposed)
            on_act()


def store_parts(eng, scratch, rt, b, buf, stored):
    for part in range(3):
        dst = scratch[8 * rt:8 * rt + 8, HD * part:HD * (part + 1), SEQ * b:SEQ * (b + 1)]
        eng.dma_start(dst, buf[:, part, :]).then_inc(stored, 16)


def load_queries(eng, dst, part_of, loaded):
    for part in range(3):
        at, times = HD * Q_PARTS.index(part), Q_PARTS.count(part)
        rows = part_of(part)
        eng.dma_start(dst[at:at + HD * times, :], rows.unsqueeze(0).to_broadcast([times] + list(rows.shape))).then_inc(loaded, 16)


def load_keys(eng, dst, rows_of, loaded):
    at = 0
    for n in (3, 2, 1):
        eng.dma_start(dst[at:at + HD * n, :], rows_of(n)).then_inc(loaded, 16)
        at += HD * n


HALVES_SWAPPED = [HD * (i // HD) + (i + HD // 2) % HD for i in range(32)]


def project(nc, sh, name, hT, q_dram, k_dram, rotary):
    UNITS = [(r, rt, c) for r in range(2) for rt in range(2) for c in range(NCHUNK)]
    N = len(UNITS)
    assert N == NT
    RING = 4
    PRING = 3
    with ExitStack() as ctx:
        sb = lambda n, s, d: ctx.enter_context(nc.sbuf_tensor(f"{name}_{n}", s, d))
        sem = ctx.enter_context(semaphores(nc, name))
        pb = lambda n, s: ctx.enter_context(nc.psum_tensor(f"{name}_{n}", s, F32))
        wv = sb("wv", [P, DH, DM], F32)
        if rotary:
            slope = sb("slope", [P, HEADS], F32)
            slope_h = sb("slope_h", [HEADS, 1], F32)
            back = sb("back", [HEADS, CHUNK], F32)
            row = sb("row", [HEADS, 3, CHUNK], F32)
            row_parts = sb("row_parts", [HEADS, 3, CHUNK], BF16)
            slopes_loaded, slope8_done = sem("slopes_loaded"), sem("slope8_done")
            row_step, rows_stored = sem("row_step"), sem("rows_stored")
            w = sb("w", [P, DH, 2 * DM], F32)
            cos = sb("cos", [P, SEQ], F32)
            sin = sb("sin", [P, SEQ], F32)
            t1 = sb("t1", [P, RING, CHUNK], F32)
            swapped = sb("swapped", [P, RING, CHUNK], F32)
        else:
            w = sb("w", [P, 2, 2, P], F32)
            flatT = sb("flatT", [P, DH, TOK], F32)
            b_col = sb("b_col", [P, DH], F32)
            b_row = sb("b_row", [P, DM], F32)
        X = sb("X", [P, RING, CHUNK], F32)
        rest = sb("rest", [P, RING, CHUNK], F32)
        parts = sb("parts", [P, PRING, 3, SEQ], BF16)
        proj = pb("proj", [P, 4, CHUNK])
        values = pb("values", [P, 4, CHUNK])
        loaded, tables = sem("loaded"), sem("tables")
        projected, taken, x_done = sem("projected"), sem("taken"), sem("x")
        swap_done, t2_done = sem("swap_done"), sem("t2_done")
        high, rest_done, mid, low = sem("high"), sem("rest"), sem("mid"), sem("low")
        stored = [sem(f"stored{m}") for m in range(PRING)]
        v_done, v_copied = sem("v_done"), sem("v_copied")
        flat_done, flat_copied = sem("flat_done"), sem("flat_copied")
        block = ctx.enter_context(nc.Block())

        def high_of(n):
            c = UNITS[n][2]
            return parts[:, n // QC % PRING, 0, CHUNK * (c % QC):CHUNK * (c % QC + 1)]

        @block.sync
        def _(sp):
            if rotary:
                sp.dma_start(w[:], sh.dram["wqk"].rearrange("(a p) n -> p a n", p=P)).then_inc(loaded, 16)
                sp.dma_start(wv[:], sh.dram["wv"].rearrange("(a p) n -> p a n", p=P)).then_inc(loaded, 16)
                sp.dma_start(cos[:], sh.dram["cos"]).then_inc(tables, 16)
                sp.dma_start(sin[:], sh.dram["sin"]).then_inc(tables, 16)
                sp.dma_start(slope[:], sh.dram["slopes"].rearrange("(a n) -> a n", a=1).to_broadcast([P, HEADS])).then_inc(slopes_loaded, 16)
                sp.dma_start(slope_h[:], sh.dram["slopes"].rearrange("(n a) -> n a", a=1)).then_inc(slopes_loaded, 16)
                sp.dma_start(back[:], sh.dram["back"]).then_inc(slopes_loaded, 16)
                sp.dma_start(sh.near_d[:], sh.dram["near_d"]).then_inc(slopes_loaded, 16)
                sp.dma_start(sh.far_d[:], sh.dram["far_d"]).then_inc(slopes_loaded, 16)
                sp.wait_ge(row_step, 7)
                for part in range(3):
                    for c in range(NCHUNK):
                        sp.dma_start(q_dram[:, STORED + part, CHUNK * c:CHUNK * (c + 1)],
                                     row_parts[:, part, :]).then_inc(rows_stored, 16)
            else:
                sp.dma_start(w[:], sh.dram["wqk_heads"].rearrange("r t p n -> p r t n")).then_inc(loaded, 16)
                sp.dma_start(wv[:], sh.dram["wb"].rearrange("(a p) n -> p a n", p=P)).then_inc(loaded, 16)
                sp.dma_start(b_col[:], sh.dram["bb_col"]).then_inc(tables, 16)
                sp.dma_start(b_row[:], sh.dram["bb"].rearrange("(o n) -> o n", o=1).to_broadcast([P, DM])).then_inc(tables, 16)
            for m in range(N // QC):
                r, rt, c = UNITS[QC * m]
                for part in (high, mid, low):
                    sp.wait_ge(part, QC * (m + 1))
                store_parts(sp, k_dram if r else q_dram, rt, c // QC, parts[:, m % PRING], stored[m % PRING])
            for m in range(PRING):
                sp.wait_ge(stored[m], len(range(m, N // QC, PRING)) * 3 * 16)
            if rotary:
                sp.wait_ge(rows_stored, 3 * NCHUNK * 16)

        @block.tensor
        def _(pe):
            pe.wait_ge(loaded, 32)
            if not rotary:
                for n in range(2 * NCHUNK):
                    rt, c = n // NCHUNK, n % NCHUNK
                    if n >= 4:
                        pe.wait_ge(flat_copied, n - 3)
                    for a in range(DH):
                        last = pe.matmul(proj[:, n % 4, :], wv[:, a, P * rt:P * (rt + 1)],
                                         hT[:, a, CHUNK * c:CHUNK * (c + 1)], start=a == 0, stop=a == DH - 1)
                    last.then_inc(flat_done, 1)
                pe.wait_ge(flat_copied, 2 * NCHUNK)
            for n, (r, rt, c) in enumerate(UNITS):
                if n >= 4:
                    pe.wait_ge(taken, n - 3)
                if rotary:
                    cols = DM * r + P * rt
                    for a in range(DH):
                        last = pe.matmul(proj[:, n % 4, :], w[:, a, cols:cols + P],
                                         hT[:, a, CHUNK * c:CHUNK * (c + 1)], start=a == 0, stop=a == DH - 1)
                else:
                    last = pe.matmul(proj[:, n % 4, :], w[:, r, rt, :],
                                     flatT[:, rt, CHUNK * c:CHUNK * (c + 1)], start=True, stop=True)
                last.then_inc(projected, 1)
                if n >= 4:
                    pe.wait_ge(v_copied, n - 3)
                for a in range(DH):
                    last = pe.matmul(values[:, n % 4, 0:DM], hT[:, a, P * n:P * (n + 1)],
                                     wv[:, a, :], start=a == 0, stop=a == DH - 1)
                last.then_inc(v_done, 1)

        @block.vector
        def _(dve):
            def split_rest(n):
                dve.wait_ge(high, n + 1)
                if n >= RING:
                    dve.wait_ge(low, n - RING + 1)
                dve.tensor_tensor(rest[:, n % RING, :], X[:, n % RING, :], high_of(n),
                                  ALU.subtract).then_inc(rest_done, 1)

            def distance_rows():
                dve.wait_ge(slopes_loaded, 80)
                dve.tensor_scalar(sh.slope8[:], slope[:], 8.0, None, ALU.mult).then_inc(slope8_done, 1)
                dve.tensor_scalar(row[:, 0, :], back[:], slope_h[:], 8.0 / SCALE_A, ALU.mult, ALU.mult).then_inc(row_step, 1)
                dve.wait_ge(row_step, 1)
                dve.tensor_scalar(row[:, 0, :], row[:, 0, :], -FAR_SHIFT / SCALE_A, None, ALU.add).then_inc(row_step, 1)
                for part in range(2):
                    dve.wait_ge(row_step, 2 + 2 * part)
                    dve.tensor_copy(row_parts[:, part, :], row[:, part, :]).then_inc(row_step, 1)
                    dve.wait_ge(row_step, 3 + 2 * part)
                    dve.tensor_tensor(row[:, part + 1, :], row[:, part, :], row_parts[:, part, :],
                                      ALU.subtract).then_inc(row_step, 1)
                dve.wait_ge(row_step, 6)
                dve.tensor_copy(row_parts[:, 2, :], row[:, 2, :]).then_inc(row_step, 1)

            if rotary:
                distance_rows()
            dve.wait_ge(tables, 32)
            for n, (r, rt, c) in enumerate(UNITS):
                now = proj[:, n % 4, :]
                dve.wait_ge(projected, n + 1)
                if rotary:
                    cols = slice(CHUNK * (c % QC), CHUNK * (c % QC + 1))
                    if n >= RING:
                        dve.wait_ge(x_done, n - RING + 1)
                    dve.stream_shuffle(swapped[:, n % RING, :], now, HALVES_SWAPPED).then_inc(swap_done, 1)
                    dve.tensor_tensor(t1[:, n % RING, :], now, cos[:, cols], ALU.mult).then_inc(taken, 1)
                    dve.wait_ge(swap_done, n + 1)
                    dve.tensor_tensor(swapped[:, n % RING, :], swapped[:, n % RING, :], sin[:, cols], ALU.mult).then_inc(t2_done, 1)
                else:
                    if n >= RING:
                        dve.wait_ge(rest_done, n - RING + 1)
                    dve.tensor_copy(X[:, n % RING, :], now).then_inc(taken, 1)
                if n >= 2:
                    split_rest(n - 2)
                if not rotary:
                    dve.wait_ge(v_done, n + 1)
                    dve.tensor_tensor(sh.V[:, n, :], values[:, n % 4, 0:DM], b_row[:], ALU.add).then_inc(v_copied, 1)
            split_rest(N - 2)
            split_rest(N - 1)

        @block.gpsimd
        def _(pool):
            def low_step(n):
                c = UNITS[n][2]
                cols = slice(CHUNK * (c % QC), CHUNK * (c % QC + 1))
                m = n // QC % PRING
                pool.wait_ge(mid, n + 1)
                pool.tensor_tensor(parts[:, m, 2, cols], rest[:, n % RING, :], parts[:, m, 1, cols],
                                   ALU.subtract).then_inc(low, 1)

            for n in range(N):
                if rotary:
                    pool.wait_ge(taken, n + 1)
                    pool.wait_ge(t2_done, n + 1)
                    if n >= RING:
                        pool.wait_ge(rest_done, n - RING + 1)
                    pool.tensor_tensor(X[:, n % RING, :], t1[:, n % RING, :], swapped[:, n % RING, :], ALU.add).then_inc(x_done, 1)
                if n >= 3:
                    low_step(n - 3)
            for n in range(N - 3, N):
                low_step(n)

        @block.scalar
        def _(act):
            def mid_step(n):
                c = UNITS[n][2]
                act.wait_ge(rest_done, n + 1)
                act.activation(parts[:, n // QC % PRING, 1, CHUNK * (c % QC):CHUNK * (c % QC + 1)], rest[:, n % RING, :],
                               ACT.Copy).then_inc(mid, 1)

            if not rotary:
                act.wait_ge(tables, 32)
                for n in range(2 * NCHUNK):
                    rt, c = n // NCHUNK, n % NCHUNK
                    act.wait_ge(flat_done, n + 1)
                    act.activation(flatT[:, rt, CHUNK * c:CHUNK * (c + 1)], proj[:, n % 4, :],
                                   ACT.Identity, bias=b_col[:, rt:rt + 1]).then_inc(flat_copied, 1)
            made = x_done if rotary else taken
            for n, (r, rt, c) in enumerate(UNITS):
                m = n // QC
                act.wait_ge(made, n + 1)
                if n % QC == 0 and m >= PRING:
                    act.wait_ge(stored[m % PRING], (m // PRING) * 3 * 16)
                act.activation(high_of(n), X[:, n % RING, :], ACT.Copy).then_inc(high, 1)
                if n >= 2:
                    mid_step(n - 2)
                if rotary:
                    act.wait_ge(v_done, n + 1)
                    act.activation(sh.V[:, n, :], values[:, n % 4, 0:DM], ACT.Copy).then_inc(v_copied, 1)
            mid_step(N - 2)
            mid_step(N - 1)


SCALE_A = HD ** -0.5
SCALE_B = DM ** -0.5
FAR_AT = [0, 0, 4, 12]
FAR = 24
SHIFT, NEAR_SHIFT, FAR_SHIFT = 16.0, 44.0, 40.0
LEAST, MOST, MOST_BEFORE = 1e-8, 1e30, 1e20


def attention(nc, sh, name, q_dram, k_dram, keys, scale, distance=False):
    NK = keys // P
    TILES = [(kt, qc) for kt in range(NK) for qc in range(QC)]
    SIZES = groups_of(len(TILES))
    G = len(SIZES)
    START = [sum(SIZES[:g]) for g in range(G)]
    G2 = 2 * G
    rows_q = ROWS_Q if distance else ROWS
    DIAG = NK if distance else 0
    assert G2 % P_SLOTS == 0 and G % 2 == 0

    def tiles_of(g):
        return TILES[START[g]:START[g] + SIZES[g]]

    def diagonal(kt, qc):
        return distance and kt // QC == qc

    def before(kt, qc):
        return distance and kt < QC * qc

    def diagonals_upto(g):
        return sum(1 for x in TILES[:START[g] + SIZES[g]] if diagonal(*x))

    with ExitStack() as ctx:
        sb = lambda n, s, d: ctx.enter_context(nc.sbuf_tensor(f"{name}_{n}", s, d))
        sem = ctx.enter_context(semaphores(nc, name))
        Q = sb("Q", [rows_q, 2, UNIT_Q], BF16)
        K = sb("K", [rows_q, 2, keys], BF16)
        V = sb("V", [P, 2, NK, VW], F32)
        VF = sb("VF", [P, 2, FAR, VW], F32) if distance else None
        near = sb("near", [P, HEADS, CHUNK], F32) if distance else None
        far = sb("far", [P, HEADS, FAR], F32) if distance else None
        probs = sb("probs", [P, P_SLOTS, GROUP, CHUNK], F32)
        sums = sb("sums", [P, 2, CHUNK], F32)
        inv = sb("inv", [P, 2, 4, 4], F32)
        S = ctx.enter_context(nc.psum_tensor(f"{name}_S", [P, 2, GROUP, CHUNK], F32))
        O = ctx.enter_context(nc.psum_tensor(f"{name}_O", [P, 2, CHUNK], F32))
        loaded = [sem("loaded0"), sem("loaded1")]
        scored, exped, weighed, used = sem("scored"), sem("exped"), sem("weighed"), sem("used")
        v_ready, out_copied, turned, inverted, normed = (
            sem("v_ready"), sem("out_copied"), sem("turned"), sem("inverted"), sem("normed"))
        filled, v_copied = sem("filled"), sem("v_copied")
        guarded = sem("guarded")
        LOADS = 16 * (7 if distance else 6)
        GUARDS = 3 if distance else 2
        CREDIT = 2
        FILLS = 4 if distance else 2

        def load(sp, h, u):
            cols = slice(UNIT_Q * u, UNIT_Q * (u + 1))
            k_cols = cols if keys == SEQ else slice(0, keys)
            load_queries(sp, Q[:, u, :], lambda part: q_dram[h, HD * part:HD * (part + 1), cols], loaded[u])
            load_keys(sp, K[:, u, :], lambda n: k_dram[h, 0:HD * n, k_cols], loaded[u])
            if distance:
                sp.dma_start(Q[ROWS:rows_q, u, :], q_dram[h, STORED:STORED + 3, cols]).then_inc(loaded[u], 16)

        with nc.Block() as block:
            @block.sync
            def _(sp):
                for u in range(2):
                    load(sp, 0, u)

            if distance:
                @block.scalar
                def _(act):
                    for h in range(HEADS):
                        act.activation(near[:, h, :], sh.near_d[:], ACT.Exp, bias=sh.shift[:, 1:2],
                                       scale=sh.slope8[:, h:h + 1])
                        act.activation(far[:, h, :], sh.far_d[:], ACT.Exp, bias=sh.shift[:, 2:3],
                                       scale=sh.slope8[:, h:h + 1])

            @block.gpsimd
            def _(pool):
                pool.memset(V[:], 0.0).then_inc(filled, 1)
                pool.wait_ge(filled, 1)
                pool.memset(V[:, :, :, HD:HD + 1], 1.0).then_inc(filled, 1)
                if distance:
                    pool.memset(VF[:], 0.0).then_inc(filled, 1)
                    pool.wait_ge(filled, 3)
                    pool.memset(VF[:, :, :, HD + 1:HD + 2], 1.0).then_inc(filled, 1)
                pool.wait_ge(filled, FILLS)
                if not distance:
                    for u in range(2):
                        pool.tensor_copy(V[:, u, :, 0:HD], sh.V[:, 0:NK, 0:HD]).then_inc(v_ready, 1)

            @block.vector
            def _(dve):
                if distance:
                    dve.memset(K[ROWS:rows_q, :, :], 1.0)
                dve.memset(sh.within[:], 1.0).then_inc(guarded, 1)
                dve.memset(inv[:], 0.0).then_inc(used, P_SLOTS)
                dve.memset(sums[:], 0.0).then_inc(normed, CREDIT)

        block = ctx.enter_context(nc.Block())
        out_v = sh.attn[:, :, :].rearrange("p (u j a) (h d) -> p u a j h d", u=2, j=4, d=HD)

        @block.sync
        def _(sp):
            with sp.Fori(0, HEADS - 1) as i:
                h = sp.snap(i + 1)
                frees = [sp.snap(i * G2 + G * (u + 1)) for u in range(2)]
                for u in range(2):
                    sp.wait_ge(scored, frees[u])
                    load(sp, h, u)

        def scores(pe, i, gg, first):
            u, g = gg // G, gg % G
            if g == 0:
                pe.wait_ge(loaded[u], i * LOADS + LOADS)
            if not (first and gg < 2):
                pe.wait_ge(exped, i * G2 + gg - 1)
            for n, (kt, qc) in enumerate(tiles_of(g)):
                r = rows_q if before(kt, qc) else ROWS
                last = pe.matmul(S[:, gg % 2, n, :], K[0:r, u, P * kt:P * (kt + 1)],
                                 Q[0:r, u, CHUNK * qc:CHUNK * (qc + 1)], start=True, stop=True)
            last.then_inc(scored, 1)

        def weigh(pe, i, gg):
            u, g = gg // G, gg % G
            if g == 0:
                pe.wait_ge(v_ready, i * 2 + u + 1)
                pe.wait_ge(normed, i * 2 + u - 1 + CREDIT)
            pe.wait_ge(exped, i * G2 + gg + 1)
            if any(diagonal(*x) for x in tiles_of(g)):
                pe.wait_ge(weighed, i * 2 * DIAG + u * DIAG + diagonals_upto(g))
            if distance and g == 0:
                pass
            for n, (kt, qc) in enumerate(tiles_of(g)):
                v = VF[:, u, FAR_AT[qc] + kt, :] if before(kt, qc) else V[:, u, kt, :]
                last = pe.matmul(O[32 * qc:32 * (qc + 1), u, :], v, probs[:, gg % P_SLOTS, n, :],
                                 start=kt == 0, stop=kt == NK - 1, skip_group_check=True)
            last.then_inc(used, 1)

        def turn(pe, i, u):
            pe.wait_ge(out_copied, i * 2 + u + 1)
            for a in range(4):
                last = pe.matmul(O[:, u, P * a:P * (a + 1)], sums[:, u, P * a:P * (a + 1)], sh.ident[:, :],
                                 is_transpose=True, start=True, stop=True, skip_group_check=True)
            last.then_inc(turned, 1)

        @block.tensor
        def _(pe):
            def head(i, last):
                for gg in range(G2):
                    ahead = gg + LEAD
                    if ahead < G2:
                        scores(pe, i, ahead, False)
                    elif not last:
                        scores(pe, i + 1, ahead - G2, False)
                    weigh(pe, i, gg)
                    if gg == G + 6:
                        turn(pe, i, 0)
                turn(pe, i, 1)

            for gg in range(LEAD):
                scores(pe, 0, gg, True)
            with pe.Fori(0, HEADS - 1) as i:
                head(i, False)
            head(HEADS - 1, True)

        @block.scalar
        def _(act):
            with act.Fori(0, HEADS) as i:
                for gg in range(G2):
                    n = SIZES[gg % G]
                    act.wait_ge(scored, i * G2 + gg + 1)
                    act.wait_ge(used, i * G2 + gg + 1)
                    act.activation(probs[:, gg % P_SLOTS, 0:n, :], S[:, gg % 2, 0:n, :], ACT.Exp,
                                   bias=sh.shift[:, 0:1], scale=scale).then_inc(exped, 1)

        @block.vector
        def _(dve):
            def copy_out(i, u):
                dve.wait_ge(used, i * G2 + G * (u + 1) + P_SLOTS)
                dve.tensor_copy(sums[:, u, :], O[:, u, :]).then_inc(out_copied, 1)

            def normalise(i, u):
                dve.wait_ge(turned, i * 2 + u + 1)
                turned_sums = O[:, u, :].rearrange("p (a j w) -> p a j w", a=4, j=4)
                dve.reciprocal(inv[:, u, :, :].rearrange("p a j -> p a j"), turned_sums[:, :, :, HD]).then_inc(inverted, 1)
                dve.wait_ge(inverted, i * 2 + u + 1)
                def within(column, limit, op):
                    dve.scalar_tensor_tensor(out=sh.within[:, :, :], in0=turned_sums[:, :, :, column], scalar=limit,
                                             in1=sh.within[:, :, :], op0=op, op1=ALU.mult).then_inc(guarded, 1)

                before = (i * 2 + u) * GUARDS
                dve.wait_ge(guarded, before + 1)
                within(HD, LEAST, ALU.is_ge)
                dve.wait_ge(guarded, before + 2)
                within(HD, MOST, ALU.is_le)
                if distance:
                    dve.wait_ge(guarded, before + 3)
                    within(HD + 1, MOST_BEFORE, ALU.is_le)
                inv_b = inv[:, u, :, :].unsqueeze(3).to_broadcast([P, 4, 4, HD])
                for a in range(4):
                    last = dve.tensor_tensor(out_v[:, u, a, :, i, :], turned_sums[:, a, :, 0:HD], inv_b[:, a],
                                             ALU.mult)
                last.then_inc(normed, 1)

            def next_values(i, u):
                src = sh.V[:, :, :].rearrange("p t (h d) -> p t h d", d=HD)
                dve.tensor_scalar(V[:, u, :, 0:HD], src[:, :, i + 1, :], 1.0, None, ALU.mult).then_inc(v_ready, 1)

            def head(i, last):
                for gg in range(G2):
                    u, g = gg // G, gg % G
                    for n, (kt, qc) in enumerate(tiles_of(g)):
                        if diagonal(kt, qc):
                            dve.wait_ge(exped, i * G2 + gg + 1)
                            a = kt % QC
                            p = probs[:, gg % P_SLOTS, n, P * a:]
                            dve.scalar_tensor_tensor(out=p, in0=p, scalar=math.exp(-NEAR_SHIFT),
                                                     in1=near[:, i, 0:CHUNK - P * a], op0=ALU.mult,
                                                     op1=ALU.mult).then_inc(weighed, 1)
                    if gg == G:
                        copy_out(i, 0)
                        if not distance and not last:
                            next_values(i, 0)
                    if gg == G + 7:
                        normalise(i, 0)
                copy_out(i, 1)
                if not distance and not last:
                    next_values(i, 1)
                normalise(i, 1)

            with dve.Fori(0, HEADS - 1) as i:
                head(i, False)
            head(HEADS - 1, True)

        if distance:
            @block.gpsimd
            def _(pool):
                def values(i, u):
                    src = sh.V[:, NK * u:NK * (u + 1), :].rearrange("p t (h d) -> p t h d", d=HD)
                    pool.tensor_copy(V[:, u, :, 0:HD], src[:, :, i, :])
                    for qc in range(1, QC):
                        at, n = FAR_AT[qc], QC * qc
                        f = far[:, i, at:at + n].unsqueeze(2)
                        pool.tensor_tensor(VF[:, u, at:at + n, 0:HD], src[:, 0:n, i, :],
                                           f.to_broadcast([P, n, HD]), ALU.mult)
                    pool.tensor_copy(VF[:, u, :, HD:HD + 1], far[:, i, :].unsqueeze(2)).then_inc(v_ready, 1)

                for u in range(2):
                    values(0, u)
                with pool.Fori(1, HEADS) as i:
                    for u in range(2):
                        pool.wait_ge(used, (i - 1) * G2 + G * (u + 1) + P_SLOTS)
                        values(i, u)


def guard(nc, sh, name, distance):
    with ExitStack() as ctx:
        sb = lambda n, s, d: ctx.enter_context(nc.sbuf_tensor(f"{name}_{n}", s, d))
        least = sb("least", [P, 2], F32)
        outside = sb("outside", [P, 1], F32)
        anywhere = sb("anywhere", [P, 1], F32)
        sem = ctx.enter_context(semaphores(nc, name))
        reduced, step = sem("reduced"), sem("step")
        block = ctx.enter_context(nc.Block())

        @block.vector
        def _(dve):
            dve.tensor_reduce(least[:, 0:1], sh.within[:, :, :], AX.XY, ALU.min).then_inc(step, 1)
            dve.wait_ge(step, 1)
            if distance:
                dve.tensor_reduce(least[:, 1:2], sh.slope8[:, :], AX.X, ALU.min).then_inc(step, 1)
                dve.wait_ge(step, 2)
                dve.scalar_tensor_tensor(out=outside[:], in0=least[:, 1:2], scalar=0.0, in1=least[:, 0:1],
                                         op0=ALU.is_ge, op1=ALU.mult).then_inc(step, 1)
                dve.wait_ge(step, 3)
                dve.tensor_scalar(outside[:], outside[:], -1.0, 1.0, ALU.mult, ALU.add).then_inc(step, 1)
            else:
                dve.tensor_scalar(outside[:], least[:, 0:1], -1.0, 1.0, ALU.mult, ALU.add).then_inc(step, 1)
            dve.wait_ge(reduced, 1)
            dve.tensor_copy(sh.flag[:], anywhere[0:1, :]).then_inc(step, 1)
            dve.wait_ge(step, 5 if distance else 3)

        @block.gpsimd
        def _(pool):
            pool.wait_ge(step, 4 if distance else 2)
            pool.partition_all_reduce(anywhere[:, :], outside[:, :], P, bass.bass_isa.ReduceOp.max).then_inc(reduced, 1)


def general_attention(nc, sh, name, q_dram, k_dram, keys, scale, distance):
    NHALF = keys // UNIT_Q
    NQUAD = keys // CHUNK
    QT = UNIT_Q // P
    with ExitStack() as ctx:
        sb = lambda n, s, d: ctx.enter_context(nc.sbuf_tensor(f"{name}_{n}", s, d))
        Q = sb("Q", [ROWS, P], BF16)
        K = sb("K", [ROWS, keys], BF16)
        L = sb("L", [P, keys], F32)
        probsT = sb("probsT", [P, 2, CHUNK], F32)
        neg_max = sb("neg_max", [P, 1], F32)
        total = sb("total", [P, 1], F32)
        inv = sb("inv", [P, 1], F32)
        ahead = sb("ahead", [P, 2 * SEQ], F32) if distance else None
        S = ctx.enter_context(nc.psum_tensor(f"{name}_S", [P, 4, CHUNK], F32))
        T = ctx.enter_context(nc.psum_tensor(f"{name}_T", [P, 2, CHUNK], F32))
        O = ctx.enter_context(nc.psum_tensor(f"{name}_O", [P, CHUNK], F32))
        sem = ctx.enter_context(semaphores(nc, name))
        loaded, scored, biased, taken, maxed, exped = (
            sem("loaded"), sem("scored"), sem("biased"), sem("taken"), sem("maxed"), sem("exped"))
        turned, copied, weighed, inverted, finished, table = (
            sem("turned"), sem("copied"), sem("weighed"), sem("inverted"), sem("finished"), sem("table"))
        with nc.Block() as block:
            @block.vector
            def _(dve):
                dve.memset(inv[:], 0.0).then_inc(finished, 1)
        block = ctx.enter_context(nc.Block())
        out_v = sh.attn[:, :, :].rearrange("p (u t) (h d) -> p u t h d", u=2, d=HD)
        v_v = sh.V[:, :, :].rearrange("p (u t) (h d) -> p u t h d", u=2, d=HD)

        def rounds(eng, body, before=None):
            flag = eng.value_load(sh.flag[0:1, 0:1], min_val=0, max_val=1)
            with eng.If(flag > 0):
                if before:
                    before()
                with eng.Fori(0, HEADS) as h:
                    with eng.Fori(0, 2) as u:
                        with eng.Fori(0, QT) as qt:
                            body(h, u, qt, eng.snap((h * 2 + u) * QT + qt))
            with eng.Else():
                pass

        @block.sync
        def _(sp):
            q_v = q_dram.rearrange("h r (u t n) -> h r u t n", u=2, n=P)
            k_v = k_dram.rearrange("h r (u n) -> h r u n", u=2)

            def load(h, u, qt, n):
                free = sp.snap(n + 1)
                sp.wait_ge(finished, free)
                load_queries(sp, Q, lambda part: q_v[h, HD * part:HD * (part + 1), u, qt, :], loaded)
                load_keys(sp, K, lambda m: k_v[h, 0:HD * m, u, :] if keys == SEQ else k_dram[h, 0:HD * m, :], loaded)

            rounds(sp, load)

        @block.tensor
        def _(pe):
            def round_(h, u, qt, n):
                pe.wait_ge(loaded, n * 96 + 96)
                for half in range(NHALF):
                    if half:
                        pe.wait_ge(taken, n * NHALF + half)
                    for j in range(4):
                        at = UNIT_Q * half + CHUNK * j
                        last = pe.matmul(S[:, j, :], Q[:, :], K[:, at:at + CHUNK], start=True, stop=True)
                    last.then_inc(scored, 1)
                pe.wait_ge(exped, n + 1)

                def weigh(quad):
                    pe.wait_ge(copied, n * NQUAD + quad + 1)
                    for j in range(4):
                        kt = 4 * quad + j
                        v = v_v[:, u, kt, h, :] if keys == SEQ else v_v[:, kt // QT, kt % QT, h, :]
                        last = pe.matmul(O[:, 0:HD], probsT[:, quad % 2, P * j:P * (j + 1)], v,
                                         start=kt == 0, stop=kt == keys // P - 1)
                    last.then_inc(weighed, 1)

                for quad in range(NQUAD):
                    for j in range(4):
                        at = CHUNK * quad + P * j
                        last = pe.matmul(T[:, quad % 2, P * j:P * (j + 1)], L[:, at:at + P], sh.ident[:, :],
                                         is_transpose=True, start=True, stop=True)
                    last.then_inc(turned, 1)
                    if quad:
                        weigh(quad - 1)
                weigh(NQUAD - 1)

            rounds(pe, round_)

        @block.scalar
        def _(act):
            def round_(h, u, qt, n):
                act.wait_ge(maxed, n + 1)
                act.activation(L[:, :], L[:, :], ACT.Exp, bias=neg_max[:, :], accum_out=total[:, :]).then_inc(exped, 1)
                for quad in range(NQUAD):
                    act.wait_ge(turned, n * NQUAD + quad + 1)
                    if quad >= 2:
                        act.wait_ge(weighed, n * NQUAD + quad - 1)
                    act.activation(probsT[:, quad % 2, :], T[:, quad % 2, :], ACT.Copy).then_inc(copied, 1)

            rounds(act, round_)

        @block.vector
        def _(dve):
            def round_(h, u, qt, n):
                if distance:
                    start = qt * -P + SEQ
                    d = ahead[:, bass.ds(start, SEQ)]
                for half in range(NHALF):
                    l = L[:, UNIT_Q * half:UNIT_Q * (half + 1)]
                    s = S[:, :, :].rearrange("p j n -> p (j n)")
                    if distance:
                        dve.wait_ge(finished, n + 1)
                        dve.tensor_scalar(l, d, sh.slope8[:, bass.ds(h, 1)], None, ALU.mult).then_inc(biased, 1)
                        dve.wait_ge(biased, n + 1)
                        dve.wait_ge(scored, n * NHALF + half + 1)
                        dve.scalar_tensor_tensor(out=l, in0=s, scalar=scale, in1=l, op0=ALU.mult,
                                                 op1=ALU.add).then_inc(taken, 1)
                    else:
                        if half == 0:
                            dve.wait_ge(finished, n + 1)
                        dve.wait_ge(scored, n * NHALF + half + 1)
                        dve.tensor_scalar(l, s, scale, None, ALU.mult).then_inc(taken, 1)
                dve.wait_ge(taken, n * NHALF + NHALF)
                dve.tensor_reduce(neg_max[:, :], L[:, :], AX.X, ALU.max, negate=True).then_inc(maxed, 1)
                dve.wait_ge(exped, n + 1)
                dve.reciprocal(inv[:, :], total[:, :]).then_inc(inverted, 1)
                dve.wait_ge(weighed, n * NQUAD + NQUAD)
                dve.wait_ge(inverted, n + 1)
                dve.tensor_scalar(out_v[:, u, qt, h, :], O[:, 0:HD], inv[:, 0:1], None, ALU.mult).then_inc(finished, 1)

            rounds(dve, round_, (lambda: dve.wait_ge(table, 2)) if distance else None)

        if distance:
            @block.gpsimd
            def _(pool):
                flag = pool.value_load(sh.flag[0:1, 0:1], min_val=0, max_val=1)
                with pool.If(flag > 0):
                    pool.iota(ahead[:, :], pattern=[[1, 2 * SEQ]], base=-SEQ, channel_multiplier=-1,
                              allow_small_or_imprecise_dtypes=True).then_inc(table, 1)
                    pool.wait_ge(table, 1)
                    pool.tensor_scalar(ahead[:, :], ahead[:, :], 0.0, None, ALU.min).then_inc(table, 1)
                with pool.Else():
                    pass


def project_out(nc, sh):
    with ExitStack() as ctx:
        sb = lambda n, s, d: ctx.enter_context(nc.sbuf_tensor("po_" + n, s, d))
        sem = ctx.enter_context(semaphores(nc, "po_"))
        w = sb("w", [P, DH, DM], F32)
        bias = sb("bias", [P, DM], F32)
        T = sb("T", [P, DH, TOK], F32)
        psum = ctx.enter_context(nc.psum_tensor("po_ps", [P, 4, CHUNK], F32))
        acc = ctx.enter_context(nc.psum_tensor("po_acc", [P, 4, CHUNK], F32))
        loaded, copied, transposed, done, added, biased = (
            sem("loaded"), sem("copied"), sem("transposed"), sem("done"), sem("added"), sem("biased"))
        block = ctx.enter_context(nc.Block())
        on_pe, on_act, steps = None, None, None

        @block.sync
        def _(sp):
            sp.dma_start(w[:], sh.dram["wo"].rearrange("(a p) n -> p a n", p=P)).then_inc(loaded, 16)
            sp.dma_start(bias[:], sh.dram["bo"].rearrange("(o n) -> o n", o=1).to_broadcast([P, DM])).then_inc(loaded, 16)

        @block.tensor
        def _(pe):
            on_pe, _, steps = transpose_steps(pe, None, sh.attn, T, sh.ident, psum, NT, lambda e, q: None,
                                              copied, transposed)
            on_pe()
            pe.wait_ge(loaded, 32)
            for t in range(NT):
                if t % 4 == 0:
                    pe.wait_ge(copied, 2 * (t // 4 + 1))
                if t >= 4:
                    pe.wait_ge(added, t - 3)
                for a in range(DH):
                    last = pe.matmul(acc[:, t % 4, 0:DM], T[:, a, P * t:P * (t + 1)], w[:, a, :],
                                     start=a == 0, stop=a == DH - 1)
                last.then_inc(done, 1)

        @block.scalar
        def _(act):
            _, on_act, _ = transpose_steps(None, act, sh.attn, T, sh.ident, psum, NT, None, copied, transposed)
            on_act()

        @block.gpsimd
        def _(pool):
            pool.wait_ge(loaded, 32)
            for t in range(NT):
                pool.tensor_tensor(sh.x[:, t, :], sh.x[:, t, :], bias[:], ALU.add).then_inc(biased, 1)

        @block.vector
        def _(dve):
            for t in range(NT):
                dve.wait_ge(done, t + 1)
                dve.wait_ge(biased, t + 1)
                dve.tensor_tensor(sh.x[:, t, :], sh.x[:, t, :], acc[:, t % 4, 0:DM], ALU.add).then_inc(added, 1)


def add_attention(nc, sh):
    with semaphores(nc, "aa") as sem:
        added = sem("added")
        with nc.Block() as block:
            @block.vector
            def _(dve):
                half = NT // 2
                for n in range(2):
                    tiles = slice(half * n, half * (n + 1))
                    dve.tensor_tensor(sh.x[:, tiles, :], sh.x[:, tiles, :], sh.attn[:, tiles, :],
                                      ALU.add).then_inc(added, 1)
                dve.wait_ge(added, 2)


def feed_forward(nc, sh, name, last_layer):
    BT = NT // BATCH
    KT = KEEP // P
    HALF = BT // 2
    NF = FF // P
    BC = KEEP // CHUNK
    CT = CHUNK // P
    TURNS = DH * KT // 4
    with ExitStack() as ctx:
        sb = lambda n, s, d: ctx.enter_context(nc.sbuf_tensor(f"{name}_{n}", s, d))
        pb = lambda n, s: ctx.enter_context(nc.psum_tensor(f"{name}_{n}", s, F32))
        sem = ctx.enter_context(semaphores(nc, name))
        w_router = sb("w_router", [P, DM], F32)
        w1 = sb("w1", [P, DH, FF], F32)
        w2 = sb("w2", [P, NF, DM], F32)
        b1 = sb("b1", [P, NF], F32)
        b2 = sb("b2", [P, DM], F32)
        stats = sb("stats", [P, NT, 6], F32)
        mv = sb("mv", [P, NT, 2], F32)
        var = sb("var", [P, NT], F32)
        std = sb("std", [P, NT], F32)
        rstd = sb("rstd", [P, NT], F32)
        hs = sb("hs", [P, NT, DM], F32)
        prod = sb("prod", [P, 2, DM], F32)
        scores = sb("scores", [P, NT], F32)
        gate = sb("gate", [P, NT], F32)
        scoresT = sb("scoresT", [BT, BATCH, P], F32)
        all_scores = sb("all_scores", [P, BATCH, SEQ], F32)
        compared = sb("compared", [P, 2, SEQ], BF16)
        tied = sb("tied", [P, 2, P], F32)
        counts = sb("counts", [P, NT, 3], F32)
        rank = sb("rank", [P, NT], F32)
        out_of = sb("out_of", [P, NT], F32)
        index = sb("index", [P, NT], U32)
        kept = sb("kept", [P, BATCH, KT, DM], F32)
        keptT = sb("keptT", [P, DH, KEEP], F32)
        hidden = sb("hidden", [P, 2, NF, CHUNK], F32)
        gathered = sb("gathered", [P, NT, DM], F32)
        up = pb("up", [P, 4, CHUNK])
        down = pb("down", [P, 4, CHUNK])
        router_loaded, w1_loaded, w2_loaded = sem("router_loaded"), sem("w1_loaded"), sem("w2_loaded")
        stats_done, mv_done, var_done, std_done = sem("stats_done"), sem("mv_done"), sem("var_done"), sem("std_done")
        rstd_done, hs_done, scored = sem("rstd_done"), sem("hs_done"), sem("scored")
        turned, scores_copied, counts_cleared = sem("turned"), sem("scores_copied"), sem("counts_cleared")
        written = [sem(f"written{b}") for b in range(BATCH)]
        spread = [sem(f"spread{b}") for b in range(BATCH)]
        counted, ranked, indexed = sem("counted"), sem("ranked"), sem("indexed")
        scattered = [sem(f"scattered{b}") for b in range(BATCH)]
        kept_loaded = [sem(f"kept_loaded{b}") for b in range(BATCH)]
        filled, drained, downed, biased = sem("filled"), sem("drained"), sem("downed"), sem("biased")
        stored = [sem(f"stored{b}") for b in range(BATCH)]
        gather_cleared = sem("gather_cleared")
        gathered_sem = [sem(f"gathered{n}") for n in range(2 * BATCH)]
        gated, summed, updated, out_done = sem("gated"), sem("summed"), sem("updated"), sem("out_done")
        block = ctx.enter_context(nc.Block())

        BANKS_B = TURNS + BC * NF

        @block.sync
        def _(sp):
            sp.dma_start(w_router[:], sh.dram["wr"].rearrange("(o n) -> o n", o=1).to_broadcast([P, DM])).then_inc(router_loaded, 16)
            sp.dma_start(w1[:], sh.dram["w1"].rearrange("(a p) n -> p a n", p=P)).then_inc(w1_loaded, 16)
            sp.dma_start(b1[:], sh.dram["b1"]).then_inc(w1_loaded, 16)
            sp.dma_start(w2[:], sh.dram["w2"].rearrange("(f p) n -> p f n", p=P)).then_inc(w2_loaded, 16)
            sp.dma_start(b2[:], sh.dram["b2"].rearrange("(o n) -> o n", o=1).to_broadcast([P, DM])).then_inc(w2_loaded, 16)

            def spread_scores(b):
                flat = sh.dram["scores"][SEQ * b:SEQ * (b + 1)]
                sp.wait_ge(scores_copied, b + 1)
                sp.dma_start(flat.rearrange("(t p) -> t p", p=P), scoresT[:, b, :]).then_inc(written[b], 16)
                sp.wait_ge(written[b], 16)
                sp.dma_start(all_scores[:, b, :], flat.rearrange("(o n) -> o n", o=1).to_broadcast([P, SEQ])).then_inc(spread[b], 16)

            def load_kept(b):
                sp.wait_ge(scattered[b], 16 * BT)
                sp.dma_start(kept[:, b, :, :], sh.dram[f"kept{b}"].rearrange("(s p) n -> p s n", p=P)).then_inc(kept_loaded[b], 16)

            def store_updates(b):
                sp.wait_ge(biased, KT * (b + 1))
                sp.dma_start(sh.dram[f"update{b}"].rearrange("(s p) n -> p s n", p=P), kept[:, b, :, :]).then_inc(stored[b], 16)

            for b in range(BATCH):
                spread_scores(b)
                load_kept(b)
            for b in range(BATCH):
                store_updates(b)
            if last_layer:
                out_v = sh.dram["out"].rearrange("(t p) c -> p t c", p=P)
                for g in range(2 * BATCH):
                    tiles = slice(HALF * g, HALF * (g + 1))
                    sp.wait_ge(updated, HALF * (g + 1))
                    sp.dma_start(out_v[:, tiles, :], sh.x[:, tiles, :]).then_inc(out_done, 16)
                sp.wait_ge(out_done, 2 * BATCH * 16)
            for b in range(BATCH):
                sp.wait_ge(stored[b], 16)

        @block.vector
        def _(dve):
            def statistics(b):
                tiles = range(BT * b, BT * (b + 1))
                for t in tiles:
                    dve.bn_stats(stats[:, t, :], sh.x[:, t, :]).then_inc(stats_done, 1)
                dve.wait_ge(stats_done, BT * (b + 1))
                for t in tiles:
                    dve.bn_aggr(mv[:, t, :], stats[:, t, :]).then_inc(mv_done, 1)
                dve.wait_ge(mv_done, BT * (b + 1))
                span = slice(BT * b, BT * (b + 1))
                dve.tensor_scalar(var[:, span], mv[:, span, 1], EPS, None, ALU.add).then_inc(var_done, 1)

            def normalise(b):
                span = slice(BT * b, BT * (b + 1))
                dve.wait_ge(std_done, b + 1)
                dve.reciprocal(rstd[:, span], std[:, span]).then_inc(rstd_done, 1)
                dve.wait_ge(rstd_done, b + 1)
                for t in range(BT * b, BT * (b + 1)):
                    dve.tensor_scalar(hs[:, t, :], sh.x[:, t, :], mv[:, t, 0:1], rstd[:, t:t + 1],
                                      ALU.subtract, ALU.mult).then_inc(hs_done, 1)

            def score(b):
                for t in range(BT * b, BT * (b + 1)):
                    dve.wait_ge(hs_done, t + 1)
                    if t >= 2:
                        dve.wait_ge(scored, t - 1)
                    dve.tensor_tensor_reduce(out=prod[:, t % 2, :], in0=hs[:, t, :], in1=w_router[:, :],
                                             scale=1.0, scalar=0.0, op0=ALU.mult, op1=ALU.add,
                                             accum_out=scores[:, t:t + 1]).then_inc(scored, 1)

            def copy_scores(b):
                dve.wait_ge(turned, b + 1)
                dve.tensor_copy(scoresT[:, b, :], down[0:BT, b, 0:P]).then_inc(scores_copied, 1)

            def count(t):
                b, at = t // BT, P * (t % BT)
                own, mine = all_scores[:, b, :], scores[:, t:t + 1]
                if t >= 2:
                    dve.wait_ge(counted, 3 * (t - 1))
                if at:
                    dve.tensor_scalar(compared[:, t % 2, 0:at], own[:, 0:at], mine, None, ALU.is_ge, ALU.add,
                                      accum_out=counts[:, t, 0:1]).then_inc(counted, 1)
                else:
                    dve.memset(compared[:, t % 2, 0:1], 0.0).then_inc(counted, 1)
                    dve.wait_ge(counted, 3 * t + 1)
                dve.tensor_scalar(compared[:, t % 2, at:SEQ], own[:, at:SEQ], mine, None, ALU.is_gt, ALU.add,
                                  accum_out=counts[:, t, 1:2]).then_inc(counted, 1)
                dve.scalar_tensor_tensor(out=tied[:, t % 2, :], in0=own[:, at:at + P], scalar=mine,
                                         in1=sh.earlier[:], op0=ALU.is_equal, op1=ALU.mult,
                                         accum_out=counts[:, t, 2:3]).then_inc(counted, 1)

            def rank_half(g):
                tiles = slice(HALF * g, HALF * (g + 1))
                for t in range(HALF * g, HALF * (g + 1)):
                    count(t)
                dve.wait_ge(counted, 3 * HALF * (g + 1))
                dve.tensor_reduce(rank[:, tiles], counts[:, tiles, :], AX.X, ALU.add).then_inc(ranked, 1)
                dve.wait_ge(ranked, 2 * g + 1)
                dve.tensor_scalar(out_of[:, tiles], rank[:, tiles], float(KEEP), float(16 * SLOTS), ALU.is_ge, ALU.mult).then_inc(ranked, 1)
                dve.wait_ge(ranked, 2 * g + 2)
                dve.tensor_tensor(index[:, tiles], rank[:, tiles], out_of[:, tiles], ALU.add).then_inc(indexed, 1)

            def sum_batch(b):
                tiles = slice(BT * b, BT * (b + 1))
                dve.tensor_tensor(sh.x[:, tiles, :], sh.x[:, tiles, :], hs[:, tiles, :], ALU.add).then_inc(summed, 1)

            def add_bias(c):
                for n in range(CT * c, CT * (c + 1)):
                    dve.wait_ge(downed, n + 1)
                    dve.tensor_tensor(kept[:, n // KT, n % KT, :], down[:, n % 4, 0:DM], b2[:], ALU.add).then_inc(biased, 1)

            def update(g):
                dve.wait_ge(gathered_sem[g], HALF * 16)
                for t in range(HALF * g, HALF * (g + 1)):
                    dve.scalar_tensor_tensor(out=sh.x[:, t, :], in0=gathered[:, t, :], scalar=gate[:, t:t + 1],
                                             in1=sh.x[:, t, :], op0=ALU.mult, op1=ALU.add).then_inc(updated, 1)

            dve.memset(counts[:], 0.0).then_inc(counts_cleared, 1)
            statistics(0)
            normalise(0)
            dve.wait_ge(router_loaded, 16)
            score(0)
            copy_scores(0)
            statistics(1)
            dve.wait_ge(counts_cleared, 1)
            dve.wait_ge(spread[0], 16)
            rank_half(0)
            rank_half(1)
            normalise(1)
            score(1)
            copy_scores(1)
            dve.wait_ge(hs_done, NT)
            sum_batch(0)
            dve.wait_ge(spread[1], 16)
            rank_half(2)
            rank_half(3)
            sum_batch(1)
            dve.wait_ge(w2_loaded, 32)
            dve.wait_ge(drained, TURNS)
            add_bias(0)
            add_bias(1)
            dve.wait_ge(drained, BANKS_B + TURNS)
            add_bias(2)
            dve.wait_ge(gated, 1)
            dve.wait_ge(summed, 2)
            update(0)
            update(1)
            add_bias(3)
            update(2)
            update(3)
            dve.wait_ge(updated, NT)

        @block.tensor
        def _(pe):
            for b in range(BATCH):
                pe.wait_ge(scored, BT * (b + 1))
                pe.matmul(down[0:BT, b, 0:P], scores[:, BT * b:BT * (b + 1)], sh.ident[:, :], is_transpose=True,
                          start=True, stop=True).then_inc(turned, 1)

            def bank(n):
                if n >= 4:
                    pe.wait_ge(drained, n - 3)
                return up[:, n % 4, :]

            def turn_kept(b):
                pe.wait_ge(kept_loaded[b], 16)
                for k in range(TURNS):
                    n = BANKS_B * b + k
                    out = bank(n)
                    a, first = k % DH, 4 * (k // DH)
                    for j in range(4):
                        last = pe.matmul(out[:, P * j:P * (j + 1)], kept[:, b, first + j, P * a:P * (a + 1)],
                                         sh.ident[:, :], is_transpose=True, start=True, stop=True)
                    last.then_inc(filled, 1)
                pe.wait_ge(drained, BANKS_B * b + TURNS)

            def up_chunk(c):
                b, at = c // BC, CHUNK * (c % BC)
                for f in range(NF):
                    out = bank(BANKS_B * b + TURNS + NF * (c % BC) + f)
                    for a in range(DH):
                        last = pe.matmul(out, w1[:, a, P * f:P * (f + 1)], keptT[:, a, at:at + CHUNK],
                                         start=a == 0, stop=a == DH - 1)
                    last.then_inc(filled, 1)

            def down_chunk(c):
                b = c // BC
                pe.wait_ge(drained, BANKS_B * b + TURNS + NF * (c % BC + 1))
                for n in range(CT * c, CT * (c + 1)):
                    if n >= 4:
                        pe.wait_ge(biased, n - 3)
                    for f in range(NF):
                        last = pe.matmul(down[:, n % 4, 0:DM], hidden[:, c % 2, f, P * (n % CT):P * (n % CT + 1)],
                                         w2[:, f, :], start=f == 0, stop=f == NF - 1)
                    last.then_inc(downed, 1)

            pe.wait_ge(w1_loaded, 32)
            pe.wait_ge(w2_loaded, 32)
            pe.wait_ge(scores_copied, BATCH)
            for b in range(BATCH):
                turn_kept(b)
                for c in range(BC * b, BC * (b + 1)):
                    up_chunk(c)
                for c in range(BC * b, BC * (b + 1)):
                    down_chunk(c)

        @block.scalar
        def _(act):
            for b in range(BATCH):
                span = slice(BT * b, BT * (b + 1))
                act.wait_ge(var_done, b + 1)
                act.activation(std[:, span], var[:, span], ACT.Sqrt).then_inc(std_done, 1)
            act.wait_ge(w1_loaded, 32)
            for b in range(BATCH):
                for k in range(TURNS):
                    n = BANKS_B * b + k
                    a, first = k % DH, 4 * (k // DH)
                    act.wait_ge(filled, n + 1)
                    act.activation(keptT[:, a, P * first:P * (first + 4)], up[:, n % 4, :], ACT.Copy).then_inc(drained, 1)
                for c in range(BC * b, BC * (b + 1)):
                    for f in range(NF):
                        n = BANKS_B * b + TURNS + NF * (c % BC) + f
                        if c >= 2 and f == 0:
                            act.wait_ge(downed, CT * (c - 1))
                        act.wait_ge(filled, n + 1)
                        act.activation(hidden[:, c % 2, f, :], up[:, n % 4, :], ACT.Gelu_apprx_tanh,
                                       bias=b1[:, f:f + 1]).then_inc(drained, 1)
                if b == 0:
                    act.wait_ge(scored, NT)
                    act.activation(gate[:], scores[:], ACT.Sigmoid).then_inc(gated, 1)

        @block.gpsimd
        def _(pool):
            pool.memset(gathered[:], 0.0).then_inc(gather_cleared, 1)
            for b in range(BATCH):
                for g in range(2 * b, 2 * b + 2):
                    pool.wait_ge(indexed, g + 1)
                    for t in range(HALF * g, HALF * (g + 1)):
                        pool.indirect_dma_start(
                            out=sh.dram[f"kept{b}"], out_offset=bass.IndirectOffsetOnAxis(index[:, t:t + 1], 0),
                            in_=hs[:, t, :], in_offset=None, bounds_check=KEEP - 1,
                            oob_is_err=False).then_inc(scattered[b], 16)
            pool.wait_ge(gather_cleared, 1)
            for b in range(BATCH):
                pool.wait_ge(stored[b], 16)
                for g in range(2 * b, 2 * b + 2):
                    for t in range(HALF * g, HALF * (g + 1)):
                        pool.indirect_dma_start(
                            out=gathered[:, t, :], out_offset=None, in_=sh.dram[f"update{b}"],
                            in_offset=bass.IndirectOffsetOnAxis(index[:, t:t + 1], 0), bounds_check=KEEP - 1,
                            oob_is_err=False).then_inc(gathered_sem[g], 16)


INPUTS = ["x", "wqk", "wv", "cos", "sin", "slopes", "near_d", "far_d", "back", "wo", "bo",
          "wb", "bb", "bb_col", "wqk_heads", "wr", "w1", "b1", "w2", "b2", "ident", "earlier"]


def build(nc, dram, stop_after=99):
    sh = Shared()
    sh.dram = dram
    with ExitStack() as ctx:
        sb = lambda n, s, d: ctx.enter_context(nc.sbuf_tensor(n, s, d))
        sh.x = sb("x", [P, NT, DM], F32)
        sh.ident = sb("ident_sb", [P, P], F32)
        sh.earlier = sb("earlier_sb", [P, P], F32)
        sh.slope8 = sb("slope8", [P, HEADS], F32)
        sh.shift = sb("shift", [P, 3], F32)
        sh.within = sb("within", [P, 4, 4], F32)
        sh.flag = sb("flag", [1, 1], I32)
        x_loaded = ctx.enter_context(nc.semaphore("x_loaded"))
        with nc.Block() as block:
            @block.sync
            def _(sp):
                sp.dma_start(sh.x[:], dram["x"].rearrange("(t p) c -> p t c", p=P)).then_inc(x_loaded, 16)
                sp.dma_start(sh.ident[:], dram["ident"]).then_inc(x_loaded, 16)
                sp.dma_start(sh.earlier[:], dram["earlier"]).then_inc(x_loaded, 16)
                sp.wait_ge(x_loaded, 48)

            @block.vector
            def _(dve):
                for n, value in enumerate((-SHIFT, NEAR_SHIFT, FAR_SHIFT)):
                    dve.memset(sh.shift[:, n:n + 1], value)
        for layer in range(2):
            with ExitStack() as actx:
                if layer == 0:
                    sh.near_d = actx.enter_context(nc.sbuf_tensor("near_d", [P, CHUNK], F32))
                    sh.far_d = actx.enter_context(nc.sbuf_tensor("far_d", [P, FAR], F32))
                sh.V = actx.enter_context(nc.sbuf_tensor(f"V{layer}", [P, NT, DM], F32))
                with nc.sbuf_tensor(f"hT{layer}", [P, DH, TOK], F32) as hT:
                    with nc.sbuf_tensor(f"h{layer}", [P, NT, DM], F32) as h:
                        layer_norm(nc, sh, f"ln{layer}", h, hT)
                    project_scope(nc, sh, layer, hT)
                sh.attn = actx.enter_context(nc.sbuf_tensor(f"attn{layer}", [P, NT, DM], F32))
                if layer == 0:
                    attention(nc, sh, "aa", dram["qa"], dram["ka"], SEQ, SCALE_A, True)
                    guard(nc, sh, "ga", True)
                    general_attention(nc, sh, "na", dram["qa"], dram["ka"], SEQ, SCALE_A, True)
                    project_out(nc, sh)
                else:
                    attention(nc, sh, "ab", dram["qb"], dram["kb"], TOK, SCALE_B)
                    guard(nc, sh, "gb", False)
                    general_attention(nc, sh, "nb", dram["qb"], dram["kb"], TOK, SCALE_B, False)
                    add_attention(nc, sh)
            if stop_after == 2 * layer:
                break
            feed_forward(nc, sh, f"ff{layer}", layer == 1)


def project_scope(nc, sh, layer, hT):
    if layer == 0:
        project(nc, sh, "pa", hT, sh.dram["qa"], sh.dram["ka"], True)
    else:
        project(nc, sh, "pb", hT, sh.dram["qb"], sh.dram["kb"], False)


def lay_out(v):
    f = lambda a: np.ascontiguousarray(np.asarray(a))
    g = {k: f(a) for k, a in v.items()}
    d = {}
    d["x"] = g["L0_attn_a_x"].reshape(TOK, DM)
    wT = g["L0_attn_a_qkv_w"].T
    d["wqk"] = wT[:, 0:2 * DM]
    d["wv"] = wT[:, 2 * DM:]
    inv_freq = (np.float32(1.0) / np.float32(10000.0) ** (np.arange(0, HD, 2, dtype=np.float32) / np.float32(HD))).astype(np.float32)
    freqs = np.arange(SEQ, dtype=np.float32)[None, :] * inv_freq[:, None]
    cos, sin = np.cos(freqs).astype(np.float32), np.sin(freqs).astype(np.float32)
    d["cos"] = np.tile(np.concatenate([cos, cos]), (P // HD, 1))
    d["sin"] = np.tile(np.concatenate([-sin, sin]), (P // HD, 1))
    d["slopes"] = g["L0_attn_a_slopes"]
    p, j = np.arange(P)[:, None], np.arange(CHUNK)[None, :]
    d["near_d"] = np.minimum(p - j, 0).astype(np.float32)
    d["far_d"] = np.concatenate([P * np.arange(QC * qc)[None, :] + p - CHUNK * qc for qc in range(1, QC)], axis=1).astype(np.float32)
    d["back"] = np.tile(-np.arange(CHUNK, dtype=np.float32), (HEADS, 1))
    d["wo"] = g["L0_attn_a_proj_w"].T
    d["bo"] = g["L0_attn_a_proj_b"]
    d["wb"] = g["L0_attn_b_proj_w"].T
    d["bb"] = g["L0_attn_b_proj_b"]
    d["bb_col"] = d["bb"].reshape(DH, P).T
    heads = np.zeros((2, 2, P, P), np.float32)
    for r, name in enumerate(("wq", "wk")):
        for h in range(HEADS):
            at = HD * (h % 8)
            heads[r, h // 8, at:at + HD, at:at + HD] = g["L0_attn_b_" + name][h]
    d["wqk_heads"] = heads
    d["wr"] = g["L0_ffn_w_router"]
    d["w1"], d["b1"], d["w2"], d["b2"] = (g["L0_ffn_" + n] for n in ("W1", "b1", "W2", "b2"))
    d["b1"] = d["b1"].reshape(FF // P, P).T
    d["ident"] = np.eye(P, dtype=np.float32)
    d["earlier"] = (np.arange(P)[None, :] < np.arange(P)[:, None]).astype(np.float32)
    return {k: np.ascontiguousarray(a) for k, a in d.items()}


SCRATCH = {"qa": ([HEADS, STORED + 3, TOK], BF16), "ka": ([HEADS, STORED, TOK], BF16),
           "qb": ([HEADS, STORED, TOK], BF16), "kb": ([HEADS, STORED, TOK], BF16),
           "scores": ([TOK], F32), "kept0": ([KEEP, DM], F32), "kept1": ([KEEP, DM], F32),
           "update0": ([KEEP, DM], F32), "update1": ([KEEP, DM], F32)}


def declare(nc, arrays):
    dram = {n: nc.dram_tensor("in_" + n, list(arrays[n].shape), mybir.dt.from_np(arrays[n].dtype),
                              kind="ExternalInput").ap() for n in INPUTS}
    dram["out"] = nc.dram_tensor("out_0", [TOK, DM], F32, kind="ExternalOutput").ap()
    for n, (shape, dt) in SCRATCH.items():
        dram[n] = nc.dram_tensor("scratch_" + n, shape, dt).ap()
    return dram


def kernel(**inputs):
    import concourse.bacc as bacc
    from concourse.bass_utils import run_bass_kernel_spmd

    arrays = lay_out(inputs)
    nc = bacc.Bacc("TRN2", target_bir_lowering=False, num_devices=1)
    build(nc, declare(nc, arrays))
    r = run_bass_kernel_spmd(nc, [{"in_" + n: arrays[n] for n in INPUTS}], core_ids=[0])
    return r.results[0]["out_0"].reshape(BATCH, SEQ, DM)
```

```python
import math
from contextlib import ExitStack, contextmanager

import numpy as np

import concourse.bass as bass
from concourse import mybir

F32 = mybir.dt.float32
BF16 = mybir.dt.bfloat16
I32 = mybir.dt.int32
U32 = mybir.dt.uint32
ALU = mybir.AluOpType
ACT = mybir.ActivationFunctionType
AX = mybir.AxisListType

P = 128
BATCH, SEQ, DM = 2, 2048, 256
TOK = BATCH * SEQ
NT = TOK // P
HEADS, HD = 16, 16
DH = DM // P
FF = 1024
KEEP = SEQ // 2
SLOTS = BATCH * KEEP
CHUNK = 512
NCHUNK = TOK // CHUNK
EPS = 1e-5

Q_PARTS = (0, 0, 0, 1, 1, 2)
K_PARTS = (0, 1, 2, 0, 1, 0)
ROWS = HD * len(Q_PARTS)
ROWS_Q = ROWS + 3
STORED = 3 * HD

UNIT_Q = 2048
QC = UNIT_Q // CHUNK
VW = 32
GROUP = 3
P_SLOTS = 4
LEAD = 2


def groups_of(tiles):
    n = -(-tiles // GROUP)
    n += -n % 2
    twos = GROUP * n - tiles
    return [GROUP] * (n - twos) + [GROUP - 1] * twos


def transpose_steps(pe, act, src, dst, ident, psum, tiles, src_ready, copied, done):
    steps = [(quad, half) for quad in range(tiles // 4) for half in range(DH)]

    def on_pe():
        for n, (quad, half) in enumerate(steps):
            if half == 0:
                src_ready(pe, quad)
            if n >= 4:
                pe.wait_ge(copied, n - 3)
            for j in range(4):
                last = pe.matmul(psum[:, n % 4, P * j:P * (j + 1)],
                                 src[:, 4 * quad + j, P * half:P * (half + 1)], ident[:, :],
                                 is_transpose=True, start=True, stop=True)
            last.then_inc(done, 1)

    def on_act():
        for n, (quad, half) in enumerate(steps):
            act.wait_ge(done, n + 1)
            act.activation(dst[:, half, CHUNK * quad:CHUNK * (quad + 1)], psum[:, n % 4, :],
                           ACT.Copy).then_inc(copied, 1)

    return on_pe, on_act, len(steps)


@contextmanager
def semaphores(nc, phase):
    taken = []

    def sem(name):
        taken.append(nc.alloc_semaphore(f"{phase}_{name}"))
        return taken[-1]

    yield sem
    nc.clear_and_free_semaphores(taken)
    nc.all_engine_barrier()


class Shared:
    pass


def statistics(dve, sh, tiles, stats_done, before=None):
    for t in tiles:
        dve.bn_stats(sh.stats[:, t, :], sh.x[:, t, :]).then_inc(stats_done, 1)
    dve.wait_ge(stats_done, (tiles.start if before is None else before) + len(tiles))
    for t in tiles:
        last = dve.bn_aggr(sh.mv[:, t, :], sh.stats[:, t, :])
    return last


def layer_norm(nc, sh, name, hs, hT):
    with ExitStack() as ctx:
        sb = lambda n, s, d: ctx.enter_context(nc.sbuf_tensor(f"{name}_{n}", s, d))
        sem = ctx.enter_context(semaphores(nc, name))
        var = sb("var", [P, NT], F32)
        std = sb("std", [P, NT], F32)
        rstd = sb("rstd", [P, NT], F32)
        psum = ctx.enter_context(nc.psum_tensor(f"{name}_ps", [P, 4, CHUNK], F32))
        var_done, std_done = sem("var"), sem("std")
        rstd_done, hs_done, copied, transposed = sem("rstd"), sem("hs"), sem("copied"), sem("tr")
        block = ctx.enter_context(nc.Block())

        @block.vector
        def _(dve):
            dve.tensor_scalar(var[:], sh.mv[:, :, 1], EPS, None, ALU.add).then_inc(var_done, 1)
            dve.wait_ge(std_done, 1)
            dve.reciprocal(rstd[:], std[:]).then_inc(rstd_done, 1)
            dve.wait_ge(rstd_done, 1)
            for t in range(NT):
                dve.tensor_scalar(hs[:, t, :], sh.x[:, t, :], sh.mv[:, t, 0:1], rstd[:, t:t + 1],
                                  ALU.subtract, ALU.mult).then_inc(hs_done, 1)

        def hs_ready(pe, quad):
            pe.wait_ge(hs_done, 4 * (quad + 1))

        @block.tensor
        def _(pe):
            on_pe, _, _ = transpose_steps(pe, None, hs, hT, sh.ident, psum, NT, hs_ready, copied, transposed)
            on_pe()

        @block.scalar
        def _(act):
            act.wait_ge(var_done, 1)
            act.activation(std[:], var[:], ACT.Sqrt).then_inc(std_done, 1)
            _, on_act, _ = transpose_steps(None, act, hs, hT, sh.ident, psum, NT, hs_ready, copied, transposed)
            on_act()


def store_parts(eng, scratch, rt, tokens, buf, stored):
    for part in range(3):
        dst = scratch[8 * rt:8 * rt + 8, HD * part:HD * (part + 1), tokens]
        eng.dma_start(dst, buf[:, part, :]).then_inc(stored, 16)


def load_queries(eng, dst, part_of, loaded):
    for part in range(3):
        at, times = HD * Q_PARTS.index(part), Q_PARTS.count(part)
        rows = part_of(part)
        eng.dma_start(dst[at:at + HD * times, :], rows.unsqueeze(0).to_broadcast([times] + list(rows.shape))).then_inc(loaded, 16)


def load_keys(eng, dst, rows_of, loaded):
    at = 0
    for n in (3, 2, 1):
        eng.dma_start(dst[at:at + HD * n, :], rows_of(n)).then_inc(loaded, 16)
        at += HD * n


HALVES_SWAPPED = [HD * (i // HD) + (i + HD // 2) % HD for i in range(32)]


def project(nc, sh, name, hT, q_dram, k_dram, rotary):
    UNITS = [(r, rt, c) for r in range(2) for rt in range(2) for c in range(NCHUNK)]
    N = len(UNITS)
    assert N == NT
    RING, ROTARY_RING = 4, 3
    SPAN = 2
    PRING = 3 if rotary else 6
    with ExitStack() as ctx:
        sb = lambda n, s, d: ctx.enter_context(nc.sbuf_tensor(f"{name}_{n}", s, d))
        sem = ctx.enter_context(semaphores(nc, name))
        pb = lambda n, s: ctx.enter_context(nc.psum_tensor(f"{name}_{n}", s, F32))
        wv = sb("wv", [P, DH, DM], F32)
        if rotary:
            slope = sb("slope", [P, HEADS], F32)
            slope_h = sb("slope_h", [HEADS, 1], F32)
            row_parts = sb("row_parts", [HEADS, 3, CHUNK], BF16)
            slopes_loaded, slope8_done = sem("slopes_loaded"), sem("slope8_done")
            row_step, rows_stored = sem("row_step"), sem("rows_stored")
            w = sb("w", [P, DH, 2 * DM], F32)
            cos = sb("cos", [P, SEQ], F32)
            sin = sb("sin", [P, SEQ], F32)
            t1 = sb("t1", [P, ROTARY_RING, CHUNK], F32)
            swapped = sb("swapped", [P, ROTARY_RING, CHUNK], F32)
        else:
            w = sb("w", [P, 2, 2, P], F32)
            flatT = sb("flatT", [P, DH, TOK], F32)
            b_col = sb("b_col", [P, DH], F32)
            b_row = sb("b_row", [P, DM], F32)
        X = sb("X", [P, RING, CHUNK], F32)
        rest = sb("rest", [P, RING, CHUNK], F32)
        if rotary:
            back, row = rest[0:HEADS, 0, :], X[0:HEADS, 0:3, :]
        parts = sb("parts", [P, PRING, 3, SPAN * CHUNK], BF16)
        proj = pb("proj", [P, 4, CHUNK])
        values = pb("values", [P, 4, CHUNK])
        loaded, tables = sem("loaded"), sem("tables")
        projected, taken, x_done = sem("projected"), sem("taken"), sem("x")
        swap_done, t2_done = sem("swap_done"), sem("t2_done")
        high, rest_done, mid, low = sem("high"), sem("rest"), sem("mid"), sem("low")
        stored = [sem(f"stored{m}") for m in range(PRING)]
        v_done, v_copied = sem("v_done"), sem("v_copied")
        flat_done, flat_copied = sem("flat_done"), sem("flat_copied")
        block = ctx.enter_context(nc.Block())

        def high_of(n):
            c = UNITS[n][2]
            return parts[:, n // SPAN % PRING, 0, CHUNK * (c % SPAN):CHUNK * (c % SPAN + 1)]

        @block.sync
        def _(sp):
            if rotary:
                sp.dma_start(w[:], sh.dram["wqk"].rearrange("(a p) n -> p a n", p=P)).then_inc(loaded, 16)
                sp.dma_start(wv[:], sh.dram["wv"].rearrange("(a p) n -> p a n", p=P)).then_inc(loaded, 16)
                sp.dma_start(cos[:], sh.dram["cos"]).then_inc(tables, 16)
                sp.dma_start(sin[:], sh.dram["sin"]).then_inc(tables, 16)
                sp.dma_start(slope[:], sh.dram["slopes"].rearrange("(a n) -> a n", a=1).to_broadcast([P, HEADS])).then_inc(slopes_loaded, 16)
                sp.dma_start(slope_h[:], sh.dram["slopes"].rearrange("(n a) -> n a", a=1)).then_inc(slopes_loaded, 16)
                sp.dma_start(back, sh.dram["back"]).then_inc(slopes_loaded, 16)
                sp.dma_start(sh.near_d[:], sh.dram["near_d"]).then_inc(slopes_loaded, 16)
                sp.dma_start(sh.far_d[:], sh.dram["far_d"]).then_inc(slopes_loaded, 16)
                sp.wait_ge(row_step, 7)
                for part in range(3):
                    for c in range(NCHUNK):
                        sp.dma_start(q_dram[:, STORED + part, CHUNK * c:CHUNK * (c + 1)],
                                     row_parts[:, part, :]).then_inc(rows_stored, 16)
            else:
                sp.dma_start(w[:], sh.dram["wqk_heads"].rearrange("r t p n -> p r t n")).then_inc(loaded, 16)
                sp.dma_start(wv[:], sh.dram["wb"].rearrange("(a p) n -> p a n", p=P)).then_inc(loaded, 16)
                sp.dma_start(b_col[:], sh.dram["bb_col"]).then_inc(tables, 16)
                sp.dma_start(b_row[:], sh.dram["bb"].rearrange("(o n) -> o n", o=1).to_broadcast([P, DM])).then_inc(tables, 16)
            for m in range(N // SPAN):
                r, rt, c = UNITS[SPAN * m]
                for part in (high, mid, low):
                    sp.wait_ge(part, SPAN * (m + 1))
                store_parts(sp, k_dram if r else q_dram, rt, slice(CHUNK * c, CHUNK * (c + SPAN)), parts[:, m % PRING], stored[m % PRING])
            for m in range(PRING):
                sp.wait_ge(stored[m], len(range(m, N // SPAN, PRING)) * 3 * 16)
            if rotary:
                sp.wait_ge(rows_stored, 3 * NCHUNK * 16)

        @block.tensor
        def _(pe):
            pe.wait_ge(loaded, 32)
            if not rotary:
                for n in range(2 * NCHUNK):
                    rt, c = n // NCHUNK, n % NCHUNK
                    if n >= 4:
                        pe.wait_ge(flat_copied, n - 3)
                    for a in range(DH):
                        last = pe.matmul(proj[:, n % 4, :], wv[:, a, P * rt:P * (rt + 1)],
                                         hT[:, a, CHUNK * c:CHUNK * (c + 1)], start=a == 0, stop=a == DH - 1)
                    last.then_inc(flat_done, 1)
                pe.wait_ge(flat_copied, 2 * NCHUNK)
            for n, (r, rt, c) in enumerate(UNITS):
                if n >= 4:
                    pe.wait_ge(taken, n - 3)
                if rotary:
                    cols = DM * r + P * rt
                    for a in range(DH):
                        last = pe.matmul(proj[:, n % 4, :], w[:, a, cols:cols + P],
                                         hT[:, a, CHUNK * c:CHUNK * (c + 1)], start=a == 0, stop=a == DH - 1)
                else:
                    last = pe.matmul(proj[:, n % 4, :], w[:, r, rt, :],
                                     flatT[:, rt, CHUNK * c:CHUNK * (c + 1)], start=True, stop=True)
                last.then_inc(projected, 1)
                if n >= 4:
                    pe.wait_ge(v_copied, n - 3)
                for a in range(DH):
                    last = pe.matmul(values[:, n % 4, 0:DM], hT[:, a, P * n:P * (n + 1)],
                                     wv[:, a, :], start=a == 0, stop=a == DH - 1)
                last.then_inc(v_done, 1)

        @block.vector
        def _(dve):
            def split_rest(n):
                dve.wait_ge(high, n + 1)
                if n >= RING:
                    dve.wait_ge(low, n - RING + 1)
                dve.tensor_tensor(rest[:, n % RING, :], X[:, n % RING, :], high_of(n),
                                  ALU.subtract).then_inc(rest_done, 1)

            def distance_rows():
                dve.wait_ge(slopes_loaded, 80)
                dve.tensor_scalar(sh.slope8[:], slope[:], 8.0, None, ALU.mult).then_inc(slope8_done, 1)
                dve.tensor_scalar(row[:, 0, :], back, slope_h[:], 8.0 / SCALE_A, ALU.mult, ALU.mult).then_inc(row_step, 1)
                dve.wait_ge(row_step, 1)
                dve.tensor_scalar(row[:, 0, :], row[:, 0, :], -FAR_SHIFT / SCALE_A, None, ALU.add).then_inc(row_step, 1)
                for part in range(2):
                    dve.wait_ge(row_step, 2 + 2 * part)
                    dve.tensor_copy(row_parts[:, part, :], row[:, part, :]).then_inc(row_step, 1)
                    dve.wait_ge(row_step, 3 + 2 * part)
                    dve.tensor_tensor(row[:, part + 1, :], row[:, part, :], row_parts[:, part, :],
                                      ALU.subtract).then_inc(row_step, 1)
                dve.wait_ge(row_step, 6)
                dve.tensor_copy(row_parts[:, 2, :], row[:, 2, :]).then_inc(row_step, 1)

            if rotary:
                distance_rows()
            dve.wait_ge(tables, 32)
            for n, (r, rt, c) in enumerate(UNITS):
                now = proj[:, n % 4, :]
                dve.wait_ge(projected, n + 1)
                if rotary:
                    cols = slice(CHUNK * (c % QC), CHUNK * (c % QC + 1))
                    if n >= ROTARY_RING:
                        dve.wait_ge(x_done, n - ROTARY_RING + 1)
                    dve.stream_shuffle(swapped[:, n % ROTARY_RING, :], now, HALVES_SWAPPED).then_inc(swap_done, 1)
                    dve.tensor_tensor(t1[:, n % ROTARY_RING, :], now, cos[:, cols], ALU.mult).then_inc(taken, 1)
                    dve.wait_ge(swap_done, n + 1)
                    dve.tensor_tensor(swapped[:, n % ROTARY_RING, :], swapped[:, n % ROTARY_RING, :], sin[:, cols], ALU.mult).then_inc(t2_done, 1)
                else:
                    if n >= RING:
                        dve.wait_ge(rest_done, n - RING + 1)
                    dve.tensor_copy(X[:, n % RING, :], now).then_inc(taken, 1)
                if n >= 2:
                    split_rest(n - 2)
                if not rotary:
                    dve.wait_ge(v_done, n + 1)
                    dve.tensor_tensor(sh.V[:, n, :], values[:, n % 4, 0:DM], b_row[:], ALU.add).then_inc(v_copied, 1)
            split_rest(N - 2)
            split_rest(N - 1)

        @block.gpsimd
        def _(pool):
            def low_step(n):
                c = UNITS[n][2]
                cols = slice(CHUNK * (c % SPAN), CHUNK * (c % SPAN + 1))
                m = n // SPAN % PRING
                pool.wait_ge(mid, n + 1)
                pool.tensor_tensor(parts[:, m, 2, cols], rest[:, n % RING, :], parts[:, m, 1, cols],
                                   ALU.subtract).then_inc(low, 1)

            for n in range(N):
                if rotary:
                    pool.wait_ge(taken, n + 1)
                    pool.wait_ge(t2_done, n + 1)
                    if n >= RING:
                        pool.wait_ge(rest_done, n - RING + 1)
                    pool.tensor_tensor(X[:, n % RING, :], t1[:, n % ROTARY_RING, :], swapped[:, n % ROTARY_RING, :], ALU.add).then_inc(x_done, 1)
                if n >= 3:
                    low_step(n - 3)
            for n in range(N - 3, N):
                low_step(n)

        @block.scalar
        def _(act):
            def mid_step(n):
                c = UNITS[n][2]
                act.wait_ge(rest_done, n + 1)
                act.activation(parts[:, n // SPAN % PRING, 1, CHUNK * (c % SPAN):CHUNK * (c % SPAN + 1)], rest[:, n % RING, :],
                               ACT.Copy).then_inc(mid, 1)

            if not rotary:
                act.wait_ge(tables, 32)
                for n in range(2 * NCHUNK):
                    rt, c = n // NCHUNK, n % NCHUNK
                    act.wait_ge(flat_done, n + 1)
                    act.activation(flatT[:, rt, CHUNK * c:CHUNK * (c + 1)], proj[:, n % 4, :],
                                   ACT.Identity, bias=b_col[:, rt:rt + 1]).then_inc(flat_copied, 1)
            made = x_done if rotary else taken
            for n, (r, rt, c) in enumerate(UNITS):
                m = n // SPAN
                act.wait_ge(made, n + 1)
                if n % SPAN == 0 and m >= PRING:
                    act.wait_ge(stored[m % PRING], (m // PRING) * 3 * 16)
                act.activation(high_of(n), X[:, n % RING, :], ACT.Copy).then_inc(high, 1)
                if n >= 2:
                    mid_step(n - 2)
                if rotary and n % 2:
                    h = n // 2
                    act.wait_ge(slope8_done, 1)
                    act.activation(sh.near[:, h, :], sh.near_d[:], ACT.Exp, bias=sh.shift[:, 1:2],
                                   scale=sh.slope8[:, h:h + 1])
                    act.activation(sh.far[:, h, :], sh.far_d[:], ACT.Exp, bias=sh.shift[:, 2:3],
                                   scale=sh.slope8[:, h:h + 1])
                if rotary:
                    act.wait_ge(v_done, n + 1)
                    act.activation(sh.V[:, n, :], values[:, n % 4, 0:DM], ACT.Copy).then_inc(v_copied, 1)
            mid_step(N - 2)
            mid_step(N - 1)


SCALE_A = HD ** -0.5
SCALE_B = DM ** -0.5
FAR_AT = [0, 0, 4, 12]
FAR = 24
SHIFT, NEAR_SHIFT, FAR_SHIFT = 16.0, 44.0, 40.0
LEAST, MOST, MOST_BEFORE = 1e-8, 1e30, 1e20


def attention(nc, sh, name, q_dram, k_dram, keys, scale, distance=False):
    NK = keys // P
    TILES = [(kt, qc) for kt in range(NK) for qc in range(QC)]
    SIZES = groups_of(len(TILES))
    G = len(SIZES)
    START = [sum(SIZES[:g]) for g in range(G)]
    G2 = 2 * G
    rows_q = ROWS_Q if distance else ROWS
    DIAG = NK if distance else 0
    assert G2 % P_SLOTS == 0 and G % 2 == 0

    def tiles_of(g):
        return TILES[START[g]:START[g] + SIZES[g]]

    def diagonal(kt, qc):
        return distance and kt // QC == qc

    def before(kt, qc):
        return distance and kt < QC * qc

    def diagonals_upto(g):
        return sum(1 for x in TILES[:START[g] + SIZES[g]] if diagonal(*x))

    with ExitStack() as ctx:
        sb = lambda n, s, d: ctx.enter_context(nc.sbuf_tensor(f"{name}_{n}", s, d))
        sem = ctx.enter_context(semaphores(nc, name))
        Q = sb("Q", [rows_q, 2, UNIT_Q], BF16)
        K = sb("K", [rows_q, 2, keys], BF16)
        V = sb("V", [P, 2, NK, VW], F32)
        VF = sb("VF", [P, 2, FAR, VW], F32) if distance else None
        near, far = sh.near, sh.far
        probs = sb("probs", [P, P_SLOTS, GROUP, CHUNK], F32)
        sums = sb("sums", [P, 2, CHUNK], F32)
        inv = sb("inv", [P, 2, 4, 4], F32)
        S = ctx.enter_context(nc.psum_tensor(f"{name}_S", [P, 2, GROUP, CHUNK], F32))
        O = ctx.enter_context(nc.psum_tensor(f"{name}_O", [P, 2, CHUNK], F32))
        loaded = [sem("loaded0"), sem("loaded1")]
        scored, exped, weighed, used = sem("scored"), sem("exped"), sem("weighed"), sem("used")
        v_ready, out_copied, turned, inverted, normed = (
            sem("v_ready"), sem("out_copied"), sem("turned"), sem("inverted"), sem("normed"))
        filled, v_copied = sem("filled"), sem("v_copied")
        guarded = sem("guarded")
        TURN_AT, COPY_AT = 6, 1
        LOADS = 16 * (7 if distance else 6)
        GUARDS = 3 if distance else 2
        CREDIT = 2
        FILLS = 5 if distance else 3

        def load(sp, h, u):
            cols = slice(UNIT_Q * u, UNIT_Q * (u + 1))
            k_cols = cols if keys == SEQ else slice(0, keys)
            load_queries(sp, Q[:, u, :], lambda part: q_dram[h, HD * part:HD * (part + 1), cols], loaded[u])
            load_keys(sp, K[:, u, :], lambda n: k_dram[h, 0:HD * n, k_cols], loaded[u])
            if distance:
                sp.dma_start(Q[ROWS:rows_q, u, :], q_dram[h, STORED:STORED + 3, cols]).then_inc(loaded[u], 16)

        with nc.Block() as block:
            @block.sync
            def _(sp):
                for u in range(2):
                    load(sp, 0, u)

            @block.gpsimd
            def _(pool):
                for u in range(2):
                    pool.memset(V[:, u, :, HD + 1:VW], 0.0).then_inc(filled, 1)
                pool.memset(V[:, :, :, HD:HD + 1], 1.0).then_inc(filled, 1)
                if distance:
                    pool.memset(VF[:], 0.0).then_inc(filled, 1)
                    pool.wait_ge(filled, 4)
                    pool.memset(VF[:, :, :, HD + 1:HD + 2], 1.0).then_inc(filled, 1)
                pool.wait_ge(filled, FILLS)

            @block.vector
            def _(dve):
                if distance:
                    dve.memset(K[ROWS:rows_q, :, :], 1.0)
                if not distance:
                    for u in range(2):
                        dve.tensor_copy(V[:, u, :, 0:HD], sh.V[:, 0:NK, 0:HD]).then_inc(v_ready, 1)
                dve.memset(sh.within[:], 1.0).then_inc(guarded, 1)
                dve.memset(inv[:], 0.0).then_inc(used, P_SLOTS)
                dve.memset(sums[:], 0.0).then_inc(normed, CREDIT)

        block = ctx.enter_context(nc.Block())
        out_v = sh.attn[:, :, :].rearrange("p (u j a) (h d) -> p u a j h d", u=2, j=4, d=HD)

        @block.sync
        def _(sp):
            with sp.Fori(0, HEADS - 1) as i:
                h = sp.snap(i + 1)
                frees = [sp.snap(i * G2 + G * (u + 1)) for u in range(2)]
                for u in range(2):
                    sp.wait_ge(scored, frees[u])
                    load(sp, h, u)

        def scores(pe, i, gg, first):
            u, g = gg // G, gg % G
            if g == 0:
                pe.wait_ge(loaded[u], i * LOADS + LOADS)
            if not (first and gg < 2):
                pe.wait_ge(exped, i * G2 + gg - 1)
            for n, (kt, qc) in enumerate(tiles_of(g)):
                r = rows_q if before(kt, qc) else ROWS
                last = pe.matmul(S[:, gg % 2, n, :], K[0:r, u, P * kt:P * (kt + 1)],
                                 Q[0:r, u, CHUNK * qc:CHUNK * (qc + 1)], start=True, stop=True)
            last.then_inc(scored, 1)

        def weigh(pe, i, gg):
            u, g = gg // G, gg % G
            if g == 0:
                pe.wait_ge(v_ready, i * 2 + u + 1)
                pe.wait_ge(normed, i * 2 + u - 1 + CREDIT)
            pe.wait_ge(exped, i * G2 + gg + 1)
            if any(diagonal(*x) for x in tiles_of(g)):
                pe.wait_ge(weighed, i * 2 * DIAG + u * DIAG + diagonals_upto(g))
            if distance and g == 0:
                pass
            for n, (kt, qc) in enumerate(tiles_of(g)):
                v = VF[:, u, FAR_AT[qc] + kt, :] if before(kt, qc) else V[:, u, kt, :]
                last = pe.matmul(O[32 * qc:32 * (qc + 1), u, :], v, probs[:, gg % P_SLOTS, n, :],
                                 start=kt == 0, stop=kt == NK - 1, skip_group_check=True)
            last.then_inc(used, 1)

        def turn(pe, i, u):
            pe.wait_ge(out_copied, i * 2 + u + 1)
            for a in range(4):
                last = pe.matmul(O[:, u, P * a:P * (a + 1)], sums[:, u, P * a:P * (a + 1)], sh.ident[:, :],
                                 is_transpose=True, start=True, stop=True, skip_group_check=True)
            last.then_inc(turned, 1)

        @block.tensor
        def _(pe):
            def head(i, first, last):
                for gg in range(G2):
                    ahead = gg + LEAD
                    if ahead < G2:
                        scores(pe, i, ahead, False)
                    elif not last:
                        scores(pe, i + 1, ahead - G2, False)
                    weigh(pe, i, gg)
                    if gg == TURN_AT and not first:
                        turn(pe, i - 1, 1)
                    if gg == G + TURN_AT:
                        turn(pe, i, 0)

            for gg in range(LEAD):
                scores(pe, 0, gg, True)
            head(0, True, False)
            with pe.Fori(1, HEADS - 1) as i:
                head(i, False, False)
            head(HEADS - 1, False, True)
            turn(pe, HEADS - 1, 1)

        @block.scalar
        def _(act):
            with act.Fori(0, HEADS) as i:
                for gg in range(G2):
                    n = SIZES[gg % G]
                    act.wait_ge(scored, i * G2 + gg + 1)
                    act.wait_ge(used, i * G2 + gg + 1)
                    act.activation(probs[:, gg % P_SLOTS, 0:n, :], S[:, gg % 2, 0:n, :], ACT.Exp,
                                   bias=sh.shift[:, 0:1], scale=scale).then_inc(exped, 1)

        @block.vector
        def _(dve):
            def copy_out(i, u):
                dve.wait_ge(used, i * G2 + G * (u + 1) + P_SLOTS)
                dve.tensor_copy(sums[:, u, :], O[:, u, :]).then_inc(out_copied, 1)

            def normalise(i, u):
                dve.wait_ge(turned, i * 2 + u + 1)
                turned_sums = O[:, u, :].rearrange("p (a j w) -> p a j w", a=4, j=4)
                dve.reciprocal(inv[:, u, :, :].rearrange("p a j -> p a j"), turned_sums[:, :, :, HD]).then_inc(inverted, 1)
                dve.wait_ge(inverted, i * 2 + u + 1)
                def within(column, limit, op):
                    dve.scalar_tensor_tensor(out=sh.within[:, :, :], in0=turned_sums[:, :, :, column], scalar=limit,
                                             in1=sh.within[:, :, :], op0=op, op1=ALU.mult).then_inc(guarded, 1)

                before = (i * 2 + u) * GUARDS
                dve.wait_ge(guarded, before + 1)
                within(HD, LEAST, ALU.is_ge)
                dve.wait_ge(guarded, before + 2)
                within(HD, MOST, ALU.is_le)
                if distance:
                    dve.wait_ge(guarded, before + 3)
                    within(HD + 1, MOST_BEFORE, ALU.is_le)
                inv_b = inv[:, u, :, :].unsqueeze(3).to_broadcast([P, 4, 4, HD])
                for a in range(4):
                    last = dve.tensor_tensor(out_v[:, u, a, :, i, :], turned_sums[:, a, :, 0:HD], inv_b[:, a],
                                             ALU.mult)
                last.then_inc(normed, 1)

            def next_values(i, u):
                src = sh.V[:, :, :].rearrange("p t (h d) -> p t h d", d=HD)
                dve.tensor_scalar(V[:, u, :, 0:HD], src[:, :, i + 1, :], 1.0, None, ALU.mult).then_inc(v_ready, 1)

            def head(i, first, last):
                for gg in range(G2):
                    u, g = gg // G, gg % G
                    for n, (kt, qc) in enumerate(tiles_of(g)):
                        if diagonal(kt, qc):
                            dve.wait_ge(exped, i * G2 + gg + 1)
                            a = kt % QC
                            p = probs[:, gg % P_SLOTS, n, P * a:]
                            dve.scalar_tensor_tensor(out=p, in0=p, scalar=math.exp(-NEAR_SHIFT),
                                                     in1=near[:, i, 0:CHUNK - P * a], op0=ALU.mult,
                                                     op1=ALU.mult).then_inc(weighed, 1)
                    if gg == COPY_AT and not first:
                        copy_out(i - 1, 1)
                        if not distance:
                            next_values(i - 1, 1)
                    if gg == TURN_AT + 1 and not first:
                        normalise(i - 1, 1)
                    if gg == G + COPY_AT:
                        copy_out(i, 0)
                        if not distance and not last:
                            next_values(i, 0)
                    if gg == G + TURN_AT + 1:
                        normalise(i, 0)

            head(0, True, False)
            with dve.Fori(1, HEADS - 1) as i:
                head(i, False, False)
            head(HEADS - 1, False, True)
            copy_out(HEADS - 1, 1)
            normalise(HEADS - 1, 1)

        if distance:
            @block.gpsimd
            def _(pool):
                def values(i, u):
                    src = sh.V[:, NK * u:NK * (u + 1), :].rearrange("p t (h d) -> p t h d", d=HD)
                    pool.tensor_copy(V[:, u, :, 0:HD], src[:, :, i, :])
                    for qc in range(1, QC):
                        at, n = FAR_AT[qc], QC * qc
                        f = far[:, i, at:at + n].unsqueeze(2)
                        pool.tensor_tensor(VF[:, u, at:at + n, 0:HD], src[:, 0:n, i, :],
                                           f.to_broadcast([P, n, HD]), ALU.mult)
                    pool.tensor_copy(VF[:, u, :, HD:HD + 1], far[:, i, :].unsqueeze(2)).then_inc(v_ready, 1)

                for u in range(2):
                    values(0, u)
                with pool.Fori(1, HEADS) as i:
                    for u in range(2):
                        pool.wait_ge(used, (i - 1) * G2 + G * (u + 1) + P_SLOTS)
                        values(i, u)


def guard(nc, sh, name, distance):
    with ExitStack() as ctx:
        sb = lambda n, s, d: ctx.enter_context(nc.sbuf_tensor(f"{name}_{n}", s, d))
        least = sb("least", [P, 2], F32)
        outside = sb("outside", [P, 1], F32)
        anywhere = sb("anywhere", [P, 1], F32)
        sem = ctx.enter_context(semaphores(nc, name))
        reduced, step = sem("reduced"), sem("step")
        block = ctx.enter_context(nc.Block())

        @block.vector
        def _(dve):
            dve.tensor_reduce(least[:, 0:1], sh.within[:, :, :], AX.XY, ALU.min).then_inc(step, 1)
            dve.wait_ge(step, 1)
            if distance:
                dve.tensor_reduce(least[:, 1:2], sh.slope8[:, :], AX.X, ALU.min).then_inc(step, 1)
                dve.wait_ge(step, 2)
                dve.scalar_tensor_tensor(out=outside[:], in0=least[:, 1:2], scalar=0.0, in1=least[:, 0:1],
                                         op0=ALU.is_ge, op1=ALU.mult).then_inc(step, 1)
                dve.wait_ge(step, 3)
                dve.tensor_scalar(outside[:], outside[:], -1.0, 1.0, ALU.mult, ALU.add).then_inc(step, 1)
            else:
                dve.tensor_scalar(outside[:], least[:, 0:1], -1.0, 1.0, ALU.mult, ALU.add).then_inc(step, 1)
            dve.wait_ge(reduced, 1)
            dve.tensor_copy(sh.flag[:], anywhere[0:1, :]).then_inc(step, 1)
            dve.wait_ge(step, 5 if distance else 3)

        @block.gpsimd
        def _(pool):
            pool.wait_ge(step, 4 if distance else 2)
            pool.partition_all_reduce(anywhere[:, :], outside[:, :], P, bass.bass_isa.ReduceOp.max).then_inc(reduced, 1)


def general_attention(nc, sh, name, q_dram, k_dram, keys, scale, distance):
    NHALF = keys // UNIT_Q
    NQUAD = keys // CHUNK
    QT = UNIT_Q // P
    with ExitStack() as ctx:
        sb = lambda n, s, d: ctx.enter_context(nc.sbuf_tensor(f"{name}_{n}", s, d))
        Q = sb("Q", [ROWS, P], BF16)
        K = sb("K", [ROWS, keys], BF16)
        L = sb("L", [P, keys], F32)
        probsT = sb("probsT", [P, 2, CHUNK], F32)
        neg_max = sb("neg_max", [P, 1], F32)
        total = sb("total", [P, 1], F32)
        inv = sb("inv", [P, 1], F32)
        ahead = sb("ahead", [P, 2 * SEQ], F32) if distance else None
        S = ctx.enter_context(nc.psum_tensor(f"{name}_S", [P, 4, CHUNK], F32))
        T = ctx.enter_context(nc.psum_tensor(f"{name}_T", [P, 2, CHUNK], F32))
        O = ctx.enter_context(nc.psum_tensor(f"{name}_O", [P, CHUNK], F32))
        sem = ctx.enter_context(semaphores(nc, name))
        loaded, scored, biased, taken, maxed, exped = (
            sem("loaded"), sem("scored"), sem("biased"), sem("taken"), sem("maxed"), sem("exped"))
        turned, copied, weighed, inverted, finished, table = (
            sem("turned"), sem("copied"), sem("weighed"), sem("inverted"), sem("finished"), sem("table"))
        with nc.Block() as block:
            @block.vector
            def _(dve):
                dve.memset(inv[:], 0.0).then_inc(finished, 1)
        block = ctx.enter_context(nc.Block())
        out_v = sh.attn[:, :, :].rearrange("p (u t) (h d) -> p u t h d", u=2, d=HD)
        v_v = sh.V[:, :, :].rearrange("p (u t) (h d) -> p u t h d", u=2, d=HD)

        def rounds(eng, body, before=None):
            flag = eng.value_load(sh.flag[0:1, 0:1], min_val=0, max_val=1)
            with eng.If(flag > 0):
                if before:
                    before()
                with eng.Fori(0, HEADS) as h:
                    with eng.Fori(0, 2) as u:
                        with eng.Fori(0, QT) as qt:
                            body(h, u, qt, eng.snap((h * 2 + u) * QT + qt))
            with eng.Else():
                pass

        @block.sync
        def _(sp):
            q_v = q_dram.rearrange("h r (u t n) -> h r u t n", u=2, n=P)
            k_v = k_dram.rearrange("h r (u n) -> h r u n", u=2)

            def load(h, u, qt, n):
                free = sp.snap(n + 1)
                sp.wait_ge(finished, free)
                load_queries(sp, Q, lambda part: q_v[h, HD * part:HD * (part + 1), u, qt, :], loaded)
                load_keys(sp, K, lambda m: k_v[h, 0:HD * m, u, :] if keys == SEQ else k_dram[h, 0:HD * m, :], loaded)

            rounds(sp, load)

        @block.tensor
        def _(pe):
            def round_(h, u, qt, n):
                pe.wait_ge(loaded, n * 96 + 96)
                for half in range(NHALF):
                    if half:
                        pe.wait_ge(taken, n * NHALF + half)
                    for j in range(4):
                        at = UNIT_Q * half + CHUNK * j
                        last = pe.matmul(S[:, j, :], Q[:, :], K[:, at:at + CHUNK], start=True, stop=True)
                    last.then_inc(scored, 1)
                pe.wait_ge(exped, n + 1)

                def weigh(quad):
                    pe.wait_ge(copied, n * NQUAD + quad + 1)
                    for j in range(4):
                        kt = 4 * quad + j
                        v = v_v[:, u, kt, h, :] if keys == SEQ else v_v[:, kt // QT, kt % QT, h, :]
                        last = pe.matmul(O[:, 0:HD], probsT[:, quad % 2, P * j:P * (j + 1)], v,
                                         start=kt == 0, stop=kt == keys // P - 1)
                    last.then_inc(weighed, 1)

                for quad in range(NQUAD):
                    for j in range(4):
                        at = CHUNK * quad + P * j
                        last = pe.matmul(T[:, quad % 2, P * j:P * (j + 1)], L[:, at:at + P], sh.ident[:, :],
                                         is_transpose=True, start=True, stop=True)
                    last.then_inc(turned, 1)
                    if quad:
                        weigh(quad - 1)
                weigh(NQUAD - 1)

            rounds(pe, round_)

        @block.scalar
        def _(act):
            def round_(h, u, qt, n):
                act.wait_ge(maxed, n + 1)
                act.activation(L[:, :], L[:, :], ACT.Exp, bias=neg_max[:, :], accum_out=total[:, :]).then_inc(exped, 1)
                for quad in range(NQUAD):
                    act.wait_ge(turned, n * NQUAD + quad + 1)
                    if quad >= 2:
                        act.wait_ge(weighed, n * NQUAD + quad - 1)
                    act.activation(probsT[:, quad % 2, :], T[:, quad % 2, :], ACT.Copy).then_inc(copied, 1)

            rounds(act, round_)

        @block.vector
        def _(dve):
            def round_(h, u, qt, n):
                if distance:
                    start = qt * -P + SEQ
                    d = ahead[:, bass.ds(start, SEQ)]
                for half in range(NHALF):
                    l = L[:, UNIT_Q * half:UNIT_Q * (half + 1)]
                    s = S[:, :, :].rearrange("p j n -> p (j n)")
                    if distance:
                        dve.wait_ge(finished, n + 1)
                        dve.tensor_scalar(l, d, sh.slope8[:, bass.ds(h, 1)], None, ALU.mult).then_inc(biased, 1)
                        dve.wait_ge(biased, n + 1)
                        dve.wait_ge(scored, n * NHALF + half + 1)
                        dve.scalar_tensor_tensor(out=l, in0=s, scalar=scale, in1=l, op0=ALU.mult,
                                                 op1=ALU.add).then_inc(taken, 1)
                    else:
                        if half == 0:
                            dve.wait_ge(finished, n + 1)
                        dve.wait_ge(scored, n * NHALF + half + 1)
                        dve.tensor_scalar(l, s, scale, None, ALU.mult).then_inc(taken, 1)
                dve.wait_ge(taken, n * NHALF + NHALF)
                dve.tensor_reduce(neg_max[:, :], L[:, :], AX.X, ALU.max, negate=True).then_inc(maxed, 1)
                dve.wait_ge(exped, n + 1)
                dve.reciprocal(inv[:, :], total[:, :]).then_inc(inverted, 1)
                dve.wait_ge(weighed, n * NQUAD + NQUAD)
                dve.wait_ge(inverted, n + 1)
                dve.tensor_scalar(out_v[:, u, qt, h, :], O[:, 0:HD], inv[:, 0:1], None, ALU.mult).then_inc(finished, 1)

            rounds(dve, round_, (lambda: dve.wait_ge(table, 2)) if distance else None)

        if distance:
            @block.gpsimd
            def _(pool):
                flag = pool.value_load(sh.flag[0:1, 0:1], min_val=0, max_val=1)
                with pool.If(flag > 0):
                    pool.iota(ahead[:, :], pattern=[[1, 2 * SEQ]], base=-SEQ, channel_multiplier=-1,
                              allow_small_or_imprecise_dtypes=True).then_inc(table, 1)
                    pool.wait_ge(table, 1)
                    pool.tensor_scalar(ahead[:, :], ahead[:, :], 0.0, None, ALU.min).then_inc(table, 1)
                with pool.Else():
                    pass


def project_out(nc, sh):
    with ExitStack() as ctx:
        sb = lambda n, s, d: ctx.enter_context(nc.sbuf_tensor("po_" + n, s, d))
        sem = ctx.enter_context(semaphores(nc, "po_"))
        w = sb("w", [P, DH, DM], F32)
        bias = sb("bias", [P, DM], F32)
        T = sb("T", [P, DH, TOK], F32)
        psum = ctx.enter_context(nc.psum_tensor("po_ps", [P, 4, CHUNK], F32))
        acc = ctx.enter_context(nc.psum_tensor("po_acc", [P, 4, CHUNK], F32))
        loaded, copied, transposed, done, added, biased = (
            sem("loaded"), sem("copied"), sem("transposed"), sem("done"), sem("added"), sem("biased"))
        stats_done = sem("stats_done")
        block = ctx.enter_context(nc.Block())
        on_pe, on_act, steps = None, None, None

        @block.sync
        def _(sp):
            sp.dma_start(w[:], sh.dram["wo"].rearrange("(a p) n -> p a n", p=P)).then_inc(loaded, 16)
            sp.dma_start(bias[:], sh.dram["bo"].rearrange("(o n) -> o n", o=1).to_broadcast([P, DM])).then_inc(loaded, 16)

        @block.tensor
        def _(pe):
            on_pe, _, steps = transpose_steps(pe, None, sh.attn, T, sh.ident, psum, NT, lambda e, q: None,
                                              copied, transposed)
            on_pe()
            pe.wait_ge(loaded, 32)
            for t in range(NT):
                if t % 4 == 0:
                    pe.wait_ge(copied, 2 * (t // 4 + 1))
                if t >= 4:
                    pe.wait_ge(added, t - 3)
                for a in range(DH):
                    last = pe.matmul(acc[:, t % 4, 0:DM], T[:, a, P * t:P * (t + 1)], w[:, a, :],
                                     start=a == 0, stop=a == DH - 1)
                last.then_inc(done, 1)

        @block.scalar
        def _(act):
            _, on_act, _ = transpose_steps(None, act, sh.attn, T, sh.ident, psum, NT, None, copied, transposed)
            on_act()

        @block.gpsimd
        def _(pool):
            pool.wait_ge(loaded, 32)
            for t in range(NT):
                pool.tensor_tensor(sh.x[:, t, :], sh.x[:, t, :], bias[:], ALU.add).then_inc(biased, 1)

        @block.vector
        def _(dve):
            for t in range(NT):
                dve.wait_ge(done, t + 1)
                dve.wait_ge(biased, t + 1)
                dve.tensor_tensor(sh.x[:, t, :], sh.x[:, t, :], acc[:, t % 4, 0:DM], ALU.add).then_inc(added, 1)
                if t % 4 == 3:
                    dve.wait_ge(added, t + 1)
                    statistics(dve, sh, range(t - 3, t + 1), stats_done)


def add_attention(nc, sh):
    with semaphores(nc, "ad") as sem:
        added, stats_done = sem("added"), sem("stats_done")
        half = NT // 2
        with nc.Block() as block:
            @block.vector
            def _(dve):
                dve.tensor_tensor(sh.x[:, 0:half, :], sh.x[:, 0:half, :], sh.attn[:, 0:half, :],
                                  ALU.add).then_inc(added, 1)
                dve.wait_ge(added, 1)
                statistics(dve, sh, range(half), stats_done)

            @block.gpsimd
            def _(pool):
                pool.tensor_tensor(sh.x[:, half:NT, :], sh.x[:, half:NT, :], sh.attn[:, half:NT, :], ALU.add)


def feed_forward(nc, sh, name, last_layer):
    BT = NT // BATCH
    KT = KEEP // P
    HALF = BT // 2
    NF = FF // P
    BC = KEEP // CHUNK
    CT = CHUNK // P
    TURNS = DH * KT // 4
    with ExitStack() as ctx:
        sb = lambda n, s, d: ctx.enter_context(nc.sbuf_tensor(f"{name}_{n}", s, d))
        pb = lambda n, s: ctx.enter_context(nc.psum_tensor(f"{name}_{n}", s, F32))
        sem = ctx.enter_context(semaphores(nc, name))
        w_router = sb("w_router", [P, DM], F32)
        w1 = sb("w1", [P, DH, FF], F32)
        w2 = sb("w2", [P, NF, DM], F32)
        b1 = sb("b1", [P, NF], F32)
        b2 = sb("b2", [P, DM], F32)
        var = sb("var", [P, NT], F32)
        std = sb("std", [P, NT], F32)
        rstd = sb("rstd", [P, NT], F32)
        W = DM + 2 if last_layer else DM
        hs = sb("hs", [P, NT, W], F32)
        prod = sb("prod", [P, 2, DM], F32)
        scores = sb("scores", [P, NT], F32)
        gate = sb("gate", [P, NT], F32)
        scoresT = sb("scoresT", [BT, BATCH, P], F32)
        all_scores = sb("all_scores", [P, BATCH, SEQ], F32)
        compared = sb("compared", [P, 2, SEQ], BF16)
        tied = sb("tied", [P, 2, P], F32)
        counts = sb("counts", [P, NT, 3], F32)
        rank = sb("rank", [P, NT], F32)
        out_of = sb("out_of", [P, NT], F32)
        index = sb("index", [P, NT], U32)
        kept = sb("kept", [P, BATCH, KT, W], F32)
        kept_gate = sb("kept_gate", [P, BATCH, KT], F32)
        kept_token = sb("kept_token", [P, BATCH, KT], U32)
        keptT = sb("keptT", [P, DH, KEEP], F32)
        hidden = sb("hidden", [P, 2, NF, CHUNK], F32)
        gathered = None if last_layer else sb("gathered", [P, NT, DM], F32)
        up = pb("up", [P, 4, CHUNK])
        down = pb("down", [P, 4, CHUNK])
        router_loaded, w1_loaded, w2_loaded = sem("router_loaded"), sem("w1_loaded"), sem("w2_loaded")
        stats_done, var_done, std_done = sem("stats_done"), sem("var_done"), sem("std_done")
        rstd_done, hs_done, scored = sem("rstd_done"), sem("hs_done"), sem("scored")
        turned, scores_copied, counts_cleared = sem("turned"), sem("scores_copied"), sem("counts_cleared")
        passed, aggregated = sem("passed"), sem("aggregated")
        written = [sem(f"written{b}") for b in range(BATCH)]
        spread = [sem(f"spread{b}") for b in range(BATCH)]
        counted, ranked, indexed = sem("counted"), sem("ranked"), sem("indexed")
        scattered = [sem(f"scattered{b}") for b in range(BATCH)]
        kept_loaded = [sem(f"kept_loaded{b}") for b in range(BATCH)]
        filled, drained, downed, biased = sem("filled"), sem("drained"), sem("downed"), sem("biased")
        stored = [sem(f"stored{b}") for b in range(BATCH)]
        gather_cleared = sem("gather_cleared")
        gathered_sem = [sem(f"gathered{n}") for n in range(2 * BATCH)]
        numbered, kept_read, scores_kept, gained = sem("numbered"), sem("kept_read"), sem("scores_kept"), sem("gained")
        base_stored = [sem(f"base_stored{b}") for b in range(BATCH)]
        gated, summed, updated, out_done = sem("gated"), sem("summed"), sem("updated"), sem("out_done")
        block = ctx.enter_context(nc.Block())

        BANKS_B = TURNS + BC * NF
        COUNTED = [2 * t + max(t - BT - 1, 0) for t in range(NT + 1)]
        RANKED = [0, 3, 6, 8, 10]
        BEHIND = DM + P

        @block.sync
        def _(sp):
            sp.dma_start(w_router[:], sh.dram["wr"].rearrange("(o n) -> o n", o=1).to_broadcast([P, DM])).then_inc(router_loaded, 16)
            sp.dma_start(w1[:], sh.dram["w1"].rearrange("(a p) n -> p a n", p=P)).then_inc(w1_loaded, 16)
            sp.dma_start(b1[:], sh.dram["b1"]).then_inc(w1_loaded, 16)
            sp.dma_start(w2[:], sh.dram["w2"].rearrange("(f p) n -> p f n", p=P)).then_inc(w2_loaded, 16)
            sp.dma_start(b2[:], sh.dram["b2"].rearrange("(o n) -> o n", o=1).to_broadcast([P, DM])).then_inc(w2_loaded, 16)

            def spread_scores(b):
                flat = sh.dram["scores"][SEQ * b:SEQ * (b + 1)]
                sp.wait_ge(scores_copied, b + 1)
                sp.dma_start(flat.rearrange("(t p) -> t p", p=P), scoresT[:, b, :]).then_inc(written[b], 16)
                sp.wait_ge(written[b], 16)
                sp.dma_start(all_scores[:, b, :], flat.rearrange("(o n) -> o n", o=1).to_broadcast([P, SEQ])).then_inc(spread[b], 16)

            def load_kept(b):
                sp.wait_ge(scattered[b], 16 * BT)
                sp.dma_start(kept[:, b, :, :], sh.dram[("last_kept" if last_layer else "kept") + str(b)].rearrange("(s p) n -> p s n", p=P)).then_inc(kept_loaded[b], 16)

            def store_updates(b):
                sp.wait_ge(biased, KT * (b + 1))
                sp.dma_start(sh.dram[f"update{b}"].rearrange("(s p) n -> p s n", p=P), kept[:, b, :, :]).then_inc(stored[b], 16)

            for b in range(BATCH):
                spread_scores(b)
                load_kept(b)
            if last_layer:
                out_v = sh.dram["out"].rearrange("(t p) c -> p t c", p=P)
                for b in range(BATCH):
                    tiles = slice(BT * b, BT * (b + 1))
                    sp.wait_ge(summed, b + 1)
                    sp.dma_start(out_v[:, tiles, :], sh.x[:, tiles, :]).then_inc(base_stored[b], 16)
                for b in range(BATCH):
                    sp.wait_ge(base_stored[b], 16)
                return
            for b in range(BATCH):
                store_updates(b)
            for b in range(BATCH):
                sp.wait_ge(stored[b], 16)

        @block.vector
        def _(dve):
            def deviations(b):
                span = slice(BT * b, BT * (b + 1))
                dve.tensor_scalar(var[:, span], sh.mv[:, span, 1], EPS, None, ALU.add).then_inc(var_done, 1)
                dve.wait_ge(std_done, b + 1)
                dve.reciprocal(rstd[:, span], std[:, span]).then_inc(rstd_done, 1)
                dve.wait_ge(rstd_done, b + 1)

            def normalise(b):
                for t in range(BT * b, BT * (b + 1)):
                    dve.tensor_scalar(hs[:, t, 0:DM], sh.x[:, t, :], sh.mv[:, t, 0:1], rstd[:, t:t + 1],
                                      ALU.subtract, ALU.mult).then_inc(hs_done, 1)

            def score(b):
                for t in range(BT * b, BT * (b + 1)):
                    dve.wait_ge(hs_done, t + 1)
                    if t >= 2:
                        dve.wait_ge(scored, t - 1)
                    dve.tensor_tensor_reduce(out=prod[:, t % 2, :], in0=hs[:, t, 0:DM], in1=w_router[:, :],
                                             scale=1.0, scalar=0.0, op0=ALU.mult, op1=ALU.add,
                                             accum_out=scores[:, t:t + 1]).then_inc(scored, 1)

            def keep_scores(b):
                tiles = slice(BT * b, BT * (b + 1))
                dve.tensor_copy(hs[:, tiles, DM], scores[:, tiles]).then_inc(scores_kept, 1)

            def copy_scores(b):
                dve.wait_ge(turned, b + 1)
                dve.tensor_copy(scoresT[:, b, :], down[0:BT, b, DM:DM + P]).then_inc(scores_copied, 1)

            def higher(t, at):
                b = t // BT
                dve.tensor_scalar(compared[:, t % 2, at:SEQ], all_scores[:, b, at:SEQ], scores[:, t:t + 1], None,
                                  ALU.is_gt, ALU.add, accum_out=counts[:, t, 1:2]).then_inc(counted, 1)

            def ties(t, at):
                dve.scalar_tensor_tensor(out=tied[:, t % 2, :], in0=all_scores[:, t // BT, at:at + P],
                                         scalar=scores[:, t:t + 1], in1=sh.earlier[:], op0=ALU.is_equal,
                                         op1=ALU.mult, accum_out=counts[:, t, 2:3]).then_inc(counted, 1)

            def count(t):
                b, at = t // BT, P * (t % BT)
                if t >= 2:
                    dve.wait_ge(counted, COUNTED[t - 1])
                    if b == 0:
                        dve.wait_ge(passed, t - 1)
                if b and at:
                    dve.tensor_scalar(compared[:, t % 2, 0:at], all_scores[:, b, 0:at], scores[:, t:t + 1], None,
                                      ALU.is_ge, ALU.add, accum_out=counts[:, t, 0:1]).then_inc(counted, 1)
                higher(t, at)
                ties(t, at)

            def rank_half(g):
                tiles = slice(HALF * g, HALF * (g + 1))
                for t in range(HALF * g, HALF * (g + 1)):
                    count(t)
                dve.wait_ge(counted, COUNTED[HALF * (g + 1)])
                dve.tensor_reduce(rank[:, tiles], counts[:, tiles, :], AX.X, ALU.add).then_inc(ranked, 1)
                if g < 2:
                    first = max(HALF * g, 1)
                    dve.wait_ge(ranked, RANKED[g] + 1)
                    dve.wait_ge(passed, min(HALF * (g + 1) - 1, BT - 1))
                    dve.tensor_tensor(rank[:, first:tiles.stop], rank[:, first:tiles.stop],
                                      down[:, 2 * g, BEHIND + first:BEHIND + tiles.stop], ALU.subtract).then_inc(ranked, 1)
                dve.wait_ge(ranked, RANKED[g + 1] - 1)
                dve.tensor_scalar(out_of[:, tiles], rank[:, tiles], float(KEEP), float(16 * SLOTS), ALU.is_ge, ALU.mult).then_inc(ranked, 1)
                dve.wait_ge(ranked, RANKED[g + 1])
                dve.tensor_tensor(index[:, tiles], rank[:, tiles], out_of[:, tiles], ALU.add).then_inc(indexed, 1)

            def sum_batch(b):
                tiles = slice(BT * b, BT * (b + 1))
                dve.tensor_tensor(sh.x[:, tiles, :], sh.x[:, tiles, :], hs[:, tiles, 0:DM], ALU.add).then_inc(summed, 1)

            def add_bias(c):
                for n in range(CT * c, CT * (c + 1)):
                    dve.wait_ge(downed, n + 1)
                    now = kept[:, n // KT, n % KT, 0:DM]
                    if last_layer:
                        dve.tensor_tensor(now, down[:, n % 4, 0:DM], b2[:], ALU.add).then_inc(gained, 1)
                        dve.wait_ge(gained, n + 1)
                        dve.tensor_scalar(now, now, kept_gate[:, n // KT, n % KT:n % KT + 1], None,
                                          ALU.mult).then_inc(biased, 1)
                    else:
                        dve.tensor_tensor(now, down[:, n % 4, 0:DM], b2[:], ALU.add).then_inc(biased, 1)

            def read_kept(b):
                dve.wait_ge(kept_loaded[b], 16)
                dve.tensor_copy(kept_token[:, b, :], kept[:, b, :, DM + 1]).then_inc(kept_read, 1)

            def update(g):
                dve.wait_ge(gathered_sem[g], HALF * 16)
                for t in range(HALF * g, HALF * (g + 1)):
                    dve.scalar_tensor_tensor(out=sh.x[:, t, :], in0=gathered[:, t, :], scalar=gate[:, t:t + 1],
                                             in1=sh.x[:, t, :], op0=ALU.mult, op1=ALU.add).then_inc(updated, 1)

            deviations(0)
            normalise(0)
            dve.wait_ge(router_loaded, 16)
            score(0)
            copy_scores(0)
            if last_layer:
                keep_scores(0)
            if last_layer:
                statistics(dve, sh, range(BT, NT), stats_done, 0).then_inc(aggregated, 1)
                dve.wait_ge(aggregated, 1)
            deviations(1)
            normalise(1)
            dve.wait_ge(counts_cleared, 1 + BT)
            dve.wait_ge(spread[0], 16)
            rank_half(0)
            rank_half(1)
            score(1)
            copy_scores(1)
            if last_layer:
                keep_scores(1)
            dve.wait_ge(hs_done, NT)
            sum_batch(0)
            dve.wait_ge(spread[1], 16)
            rank_half(2)
            rank_half(3)
            dve.wait_ge(w2_loaded, 32)
            dve.wait_ge(drained, TURNS)
            if last_layer:
                read_kept(0)
                dve.wait_ge(gated, 1)
            add_bias(0)
            add_bias(1)
            sum_batch(1)
            dve.wait_ge(drained, BANKS_B + TURNS)
            if last_layer:
                read_kept(1)
                dve.wait_ge(gated, 2)
                add_bias(2)
                add_bias(3)
                dve.wait_ge(biased, BATCH * KT)
                return
            add_bias(2)
            dve.wait_ge(gated, 1)
            dve.wait_ge(summed, 2)
            update(0)
            update(1)
            add_bias(3)
            if not last_layer:
                dve.wait_ge(updated, BT)
                statistics(dve, sh, range(0, BT), stats_done)
            for g in (2, 3):
                update(g)
                if not last_layer:
                    dve.wait_ge(updated, HALF * (g + 1))
                    statistics(dve, sh, range(HALF * g, HALF * (g + 1)), stats_done)
            dve.wait_ge(updated, NT)

        @block.tensor
        def _(pe):
            def turn_scores(b):
                pe.wait_ge(scored, BT * (b + 1))
                pe.matmul(down[0:BT, b, DM:DM + P], scores[:, BT * b:BT * (b + 1)], sh.ident[:, :],
                          is_transpose=True, start=True, stop=True).then_inc(turned, 1)

            turn_scores(0)
            for t in range(BT - 1):
                pe.wait_ge(counted, COUNTED[t + 1] - 1)
                if t == 0:
                    for bank_of_half in (0, 2):
                        pe.matmul(down[:, bank_of_half, BEHIND:BEHIND + BT], compared[:, 0, 0:P], sh.zeros[:, :],
                                  start=True, stop=False, skip_group_check=True)
                for later in range(t + 1, BT):
                    last = pe.matmul(down[:, later // HALF * 2, BEHIND + later:BEHIND + later + 1],
                                     compared[:, t % 2, P * later:P * (later + 1)], sh.ones[:, :],
                                     start=False, stop=t == later - 1, skip_group_check=True)
                last.then_inc(passed, 1)
            turn_scores(1)

            def bank(n):
                if n >= 4:
                    pe.wait_ge(drained, n - 3)
                return up[:, n % 4, :]

            def turn_kept(b):
                pe.wait_ge(kept_loaded[b], 16)
                for k in range(TURNS):
                    n = BANKS_B * b + k
                    out = bank(n)
                    a, first = k % DH, 4 * (k // DH)
                    for j in range(4):
                        last = pe.matmul(out[:, P * j:P * (j + 1)], kept[:, b, first + j, P * a:P * (a + 1)],
                                         sh.ident[:, :], is_transpose=True, start=True, stop=True)
                    last.then_inc(filled, 1)
                pe.wait_ge(drained, BANKS_B * b + TURNS)

            def up_chunk(c):
                b, at = c // BC, CHUNK * (c % BC)
                for f in range(NF):
                    out = bank(BANKS_B * b + TURNS + NF * (c % BC) + f)
                    for a in range(DH):
                        last = pe.matmul(out, w1[:, a, P * f:P * (f + 1)], keptT[:, a, at:at + CHUNK],
                                         start=a == 0, stop=a == DH - 1)
                    last.then_inc(filled, 1)

            def down_chunk(c):
                b = c // BC
                pe.wait_ge(drained, BANKS_B * b + TURNS + NF * (c % BC + 1))
                for n in range(CT * c, CT * (c + 1)):
                    if n >= 4:
                        pe.wait_ge(biased, n - 3)
                    for f in range(NF):
                        last = pe.matmul(down[:, n % 4, 0:DM], hidden[:, c % 2, f, P * (n % CT):P * (n % CT + 1)],
                                         w2[:, f, :], start=f == 0, stop=f == NF - 1)
                    last.then_inc(downed, 1)

            pe.wait_ge(w1_loaded, 32)
            pe.wait_ge(w2_loaded, 32)
            pe.wait_ge(scores_copied, BATCH)
            for b in range(BATCH):
                turn_kept(b)
                for c in range(BC * b, BC * (b + 1)):
                    up_chunk(c)
                for c in range(BC * b, BC * (b + 1)):
                    down_chunk(c)

        @block.scalar
        def _(act):
            for b in range(BATCH):
                span = slice(BT * b, BT * (b + 1))
                act.wait_ge(var_done, b + 1)
                act.activation(std[:, span], var[:, span], ACT.Sqrt).then_inc(std_done, 1)
            act.wait_ge(w1_loaded, 32)
            for b in range(BATCH):
                if last_layer:
                    act.wait_ge(kept_loaded[b], 16)
                    act.activation(kept_gate[:, b, :], kept[:, b, :, DM], ACT.Sigmoid).then_inc(gated, 1)
                for k in range(TURNS):
                    n = BANKS_B * b + k
                    a, first = k % DH, 4 * (k // DH)
                    act.wait_ge(filled, n + 1)
                    act.activation(keptT[:, a, P * first:P * (first + 4)], up[:, n % 4, :], ACT.Copy).then_inc(drained, 1)
                for c in range(BC * b, BC * (b + 1)):
                    for f in range(NF):
                        n = BANKS_B * b + TURNS + NF * (c % BC) + f
                        if c >= 2 and f == 0:
                            act.wait_ge(downed, CT * (c - 1))
                        act.wait_ge(filled, n + 1)
                        act.activation(hidden[:, c % 2, f, :], up[:, n % 4, :], ACT.Gelu_apprx_tanh,
                                       bias=b1[:, f:f + 1]).then_inc(drained, 1)
                if b == 0 and not last_layer:
                    act.wait_ge(scored, NT)
                    act.activation(gate[:], scores[:], ACT.Sigmoid).then_inc(gated, 1)

        @block.gpsimd
        def _(pool):
            if last_layer:
                pool.iota(hs[:, :, DM + 1:W], pattern=[[P, NT], [0, 1]], base=0, channel_multiplier=1,
                          allow_small_or_imprecise_dtypes=True).then_inc(numbered, 1)
            pool.memset(counts[:], 0.0).then_inc(counts_cleared, 1)
            pool.wait_ge(counts_cleared, 1)
            for t in range(BT):
                pool.memset(counts[:, t, 0:1], float(P * t)).then_inc(counts_cleared, 1)
            if last_layer:
                pool.wait_ge(numbered, 1)
            else:
                pool.memset(gathered[:], 0.0).then_inc(gather_cleared, 1)
            for b in range(BATCH):
                if last_layer:
                    pool.wait_ge(scores_kept, b + 1)
                for g in range(2 * b, 2 * b + 2):
                    pool.wait_ge(indexed, g + 1)
                    for t in range(HALF * g, HALF * (g + 1)):
                        pool.indirect_dma_start(
                            out=sh.dram[("last_kept" if last_layer else "kept") + str(b)], out_offset=bass.IndirectOffsetOnAxis(index[:, t:t + 1], 0),
                            in_=hs[:, t, :], in_offset=None, bounds_check=KEEP - 1,
                            oob_is_err=False).then_inc(scattered[b], 16)
            if last_layer:
                for n in range(BATCH * KT):
                    b = n // KT
                    if n % KT == 0:
                        pool.wait_ge(base_stored[b], 16)
                        pool.wait_ge(kept_read, b + 1)
                    pool.wait_ge(biased, n + 1)
                    pool.indirect_dma_start(
                        out=sh.dram["out"], out_offset=bass.IndirectOffsetOnAxis(kept_token[:, b, n % KT:n % KT + 1], 0),
                        in_=kept[:, b, n % KT, 0:DM], in_offset=None, bounds_check=TOK - 1,
                        compute_op=ALU.add).then_inc(out_done, 16)
                pool.wait_ge(out_done, BATCH * KT * 16)
                return
            pool.wait_ge(gather_cleared, 1)
            for b in range(BATCH):
                pool.wait_ge(stored[b], 16)
                for g in range(2 * b, 2 * b + 2):
                    for t in range(HALF * g, HALF * (g + 1)):
                        pool.indirect_dma_start(
                            out=gathered[:, t, :], out_offset=None, in_=sh.dram[f"update{b}"],
                            in_offset=bass.IndirectOffsetOnAxis(index[:, t:t + 1], 0), bounds_check=KEEP - 1,
                            oob_is_err=False).then_inc(gathered_sem[g], 16)


INPUTS = ["x", "wqk", "wv", "cos", "sin", "slopes", "near_d", "far_d", "back", "wo", "bo",
          "wb", "bb", "bb_col", "wqk_heads", "wr", "w1", "b1", "w2", "b2", "ident", "earlier"]


def load_tokens(nc, sh):
    PARTS = 4
    with semaphores(nc, "load") as sem:
        part_loaded = [sem(f"part_loaded{n}") for n in range(PARTS)]
        constants_loaded, stats_done = sem("constants_loaded"), sem("stats_done")
        tiles = [range(NT // PARTS * n, NT // PARTS * (n + 1)) for n in range(PARTS)]
        with nc.Block() as block:
            @block.sync
            def _(sp):
                x_v = sh.dram["x"].rearrange("(t p) c -> p t c", p=P)
                for n in range(PARTS):
                    span = slice(tiles[n].start, tiles[n].stop)
                    sp.dma_start(sh.x[:, span, :], x_v[:, span, :]).then_inc(part_loaded[n], 16)
                sp.dma_start(sh.ident[:], sh.dram["ident"]).then_inc(constants_loaded, 16)
                sp.dma_start(sh.earlier[:], sh.dram["earlier"]).then_inc(constants_loaded, 16)
                sp.wait_ge(constants_loaded, 32)

            @block.vector
            def _(dve):
                for n, value in enumerate((-SHIFT, NEAR_SHIFT, FAR_SHIFT)):
                    dve.memset(sh.shift[:, n:n + 1], value)
                dve.memset(sh.ones[:], 1.0)
                dve.memset(sh.zeros[:], 0.0)
                for n in range(PARTS):
                    dve.wait_ge(part_loaded[n], 16)
                    statistics(dve, sh, tiles[n], stats_done)


def build(nc, dram, stop_after=99):
    sh = Shared()
    sh.dram = dram
    with ExitStack() as ctx:
        sb = lambda n, s, d: ctx.enter_context(nc.sbuf_tensor(n, s, d))
        sh.x = sb("x", [P, NT, DM], F32)
        sh.ident = sb("ident_sb", [P, P], F32)
        sh.earlier = sb("earlier_sb", [P, P], F32)
        sh.slope8 = sb("slope8", [P, HEADS], F32)
        sh.shift = sb("shift", [P, 3], F32)
        sh.stats = sb("stats", [P, NT, 6], F32)
        sh.mv = sb("mv", [P, NT, 2], F32)
        sh.ones = sb("ones", [P, 1], BF16)
        sh.zeros = sb("zeros", [P, NT // BATCH], BF16)
        sh.within = sb("within", [P, 4, 4], F32)
        sh.flag = sb("flag", [1, 1], I32)
        load_tokens(nc, sh)
        for layer in range(2):
            with ExitStack() as actx:
                if layer == 0:
                    sh.near_d = actx.enter_context(nc.sbuf_tensor("near_d", [P, CHUNK], F32))
                    sh.far_d = actx.enter_context(nc.sbuf_tensor("far_d", [P, FAR], F32))
                    sh.near = actx.enter_context(nc.sbuf_tensor("near", [P, HEADS, CHUNK], F32))
                    sh.far = actx.enter_context(nc.sbuf_tensor("far", [P, HEADS, FAR], F32))
                sh.V = actx.enter_context(nc.sbuf_tensor(f"V{layer}", [P, NT, DM], F32))
                with nc.sbuf_tensor(f"hT{layer}", [P, DH, TOK], F32) as hT:
                    with nc.sbuf_tensor(f"h{layer}", [P, NT, DM], F32) as h:
                        layer_norm(nc, sh, f"ln{layer}", h, hT)
                    project_scope(nc, sh, layer, hT)
                sh.attn = actx.enter_context(nc.sbuf_tensor(f"attn{layer}", [P, NT, DM], F32))
                if layer == 0:
                    attention(nc, sh, "aa", dram["qa"], dram["ka"], SEQ, SCALE_A, True)
                    guard(nc, sh, "ga", True)
                    general_attention(nc, sh, "na", dram["qa"], dram["ka"], SEQ, SCALE_A, True)
                    project_out(nc, sh)
                else:
                    attention(nc, sh, "ab", dram["qb"], dram["kb"], TOK, SCALE_B)
                    guard(nc, sh, "gb", False)
                    general_attention(nc, sh, "nb", dram["qb"], dram["kb"], TOK, SCALE_B, False)
                    add_attention(nc, sh)
            if stop_after == 2 * layer:
                break
            feed_forward(nc, sh, f"ff{layer}", layer == 1)


def project_scope(nc, sh, layer, hT):
    if layer == 0:
        project(nc, sh, "pa", hT, sh.dram["qa"], sh.dram["ka"], True)
    else:
        project(nc, sh, "pb", hT, sh.dram["qb"], sh.dram["kb"], False)


def lay_out(v):
    f = lambda a: np.ascontiguousarray(np.asarray(a))
    g = {k: f(a) for k, a in v.items()}
    d = {}
    d["x"] = g["L0_attn_a_x"].reshape(TOK, DM)
    wT = g["L0_attn_a_qkv_w"].T
    d["wqk"] = wT[:, 0:2 * DM]
    d["wv"] = wT[:, 2 * DM:]
    inv_freq = (np.float32(1.0) / np.float32(10000.0) ** (np.arange(0, HD, 2, dtype=np.float32) / np.float32(HD))).astype(np.float32)
    freqs = np.arange(SEQ, dtype=np.float32)[None, :] * inv_freq[:, None]
    cos, sin = np.cos(freqs).astype(np.float32), np.sin(freqs).astype(np.float32)
    d["cos"] = np.tile(np.concatenate([cos, cos]), (P // HD, 1))
    d["sin"] = np.tile(np.concatenate([-sin, sin]), (P // HD, 1))
    d["slopes"] = g["L0_attn_a_slopes"]
    p, j = np.arange(P)[:, None], np.arange(CHUNK)[None, :]
    d["near_d"] = np.minimum(p - j, 0).astype(np.float32)
    d["far_d"] = np.concatenate([P * np.arange(QC * qc)[None, :] + p - CHUNK * qc for qc in range(1, QC)], axis=1).astype(np.float32)
    d["back"] = np.tile(-np.arange(CHUNK, dtype=np.float32), (HEADS, 1))
    d["wo"] = g["L0_attn_a_proj_w"].T
    d["bo"] = g["L0_attn_a_proj_b"]
    d["wb"] = g["L0_attn_b_proj_w"].T
    d["bb"] = g["L0_attn_b_proj_b"]
    d["bb_col"] = d["bb"].reshape(DH, P).T
    heads = np.zeros((2, 2, P, P), np.float32)
    for r, name in enumerate(("wq", "wk")):
        for h in range(HEADS):
            at = HD * (h % 8)
            heads[r, h // 8, at:at + HD, at:at + HD] = g["L0_attn_b_" + name][h]
    d["wqk_heads"] = heads
    d["wr"] = g["L0_ffn_w_router"]
    d["w1"], d["b1"], d["w2"], d["b2"] = (g["L0_ffn_" + n] for n in ("W1", "b1", "W2", "b2"))
    d["b1"] = d["b1"].reshape(FF // P, P).T
    d["ident"] = np.eye(P, dtype=np.float32)
    d["earlier"] = (np.arange(P)[None, :] < np.arange(P)[:, None]).astype(np.float32)
    return {k: np.ascontiguousarray(a) for k, a in d.items()}


SCRATCH = {"qa": ([HEADS, STORED + 3, TOK], BF16), "ka": ([HEADS, STORED, TOK], BF16),
           "qb": ([HEADS, STORED, TOK], BF16), "kb": ([HEADS, STORED, TOK], BF16),
           "scores": ([TOK], F32), "kept0": ([KEEP, DM], F32), "kept1": ([KEEP, DM], F32),
           "last_kept0": ([KEEP, DM + 2], F32), "last_kept1": ([KEEP, DM + 2], F32),
           "update0": ([KEEP, DM], F32), "update1": ([KEEP, DM], F32)}


def declare(nc, arrays):
    dram = {n: nc.dram_tensor("in_" + n, list(arrays[n].shape), mybir.dt.from_np(arrays[n].dtype),
                              kind="ExternalInput").ap() for n in INPUTS}
    dram["out"] = nc.dram_tensor("out_0", [TOK, DM], F32, kind="ExternalOutput").ap()
    for n, (shape, dt) in SCRATCH.items():
        dram[n] = nc.dram_tensor("scratch_" + n, shape, dt).ap()
    return dram


def kernel(**inputs):
    import concourse.bacc as bacc
    from concourse.bass_utils import run_bass_kernel_spmd

    arrays = lay_out(inputs)
    nc = bacc.Bacc("TRN2", target_bir_lowering=False, num_devices=1)
    build(nc, declare(nc, arrays))
    r = run_bass_kernel_spmd(nc, [{"in_" + n: arrays[n] for n in INPUTS}], core_ids=[0])
    return r.results[0]["out_0"].reshape(BATCH, SEQ, DM)
```
